# Optimizing a Trainium2 kernel written in Bass

```python
import numpy as np
import jax
import jax.numpy as jnp

def _softmax(x, axis=-1):
    return jax.nn.softmax(x, axis=axis)

def _gelu(x):
    return jax.nn.gelu(x, approximate=True)

def _silu(x):
    return jax.nn.silu(x)

def _sigmoid(x):
    return jax.nn.sigmoid(x)

def _layernorm(x, axis=-1, eps=1e-05):
    m = jnp.mean(x, axis=axis, keepdims=True)
    v = jnp.var(x, axis=axis, keepdims=True)
    return (x - m) / jnp.sqrt(v + eps)

def _scatter_add(tgt, idx, src, axis=0):
    return tgt.at[idx].add(src)

def _segment_sum(src, seg, n):
    return jax.ops.segment_sum(src, seg, n)
kernel_name = 'mk_seq_preln_d1_jaxref_r4_b99a35'

def setup_inputs(seed: int=0):
    np.random.seed(seed)
    _w = jnp.asarray

    def _L0_attn_setup():
        import jax, jax.numpy as jnp
        import numpy as np
        DIM, H, KV, HD, WIN = (256, 16, 4, 64, 128)
        EPS = 1e-06

        def rmsnorm(x, w, eps=EPS):
            return x * jax.lax.rsqrt(jnp.mean(x * x, axis=-1, keepdims=True) + eps) * w
        key = jax.random.key(seed)
        ks = jax.random.split(key, 7)
        B, T = (4, 512)
        s = 0.02
        return {'x': jax.random.normal(ks[0], (B, T, DIM), dtype=jnp.float32), 'wq': jax.random.normal(ks[1], (H * HD, DIM), dtype=jnp.float32) * s, 'wk': jax.random.normal(ks[2], (KV * HD, DIM), dtype=jnp.float32) * s, 'wv': jax.random.normal(ks[3], (KV * HD, DIM), dtype=jnp.float32) * s, 'wo': jax.random.normal(ks[4], (DIM, H * HD), dtype=jnp.float32) * s, 'q_norm_w': jnp.ones((HD,), dtype=jnp.float32), 'k_norm_w': jnp.ones((HD,), dtype=jnp.float32)}
    _L0_attn_in = _L0_attn_setup()

    def _L0_ffn_setup():
        import jax, jax.numpy as jnp
        import numpy as np
        key = jax.random.key(seed)
        ks = jax.random.split(key, 5)
        B, S, D_in, D_out, E, R = (4, 256, 256, 256, 8, 16)
        x = jax.random.normal(ks[0], (B, S, D_in), dtype=jnp.float32)
        weight = jax.random.normal(ks[1], (D_out, D_in), dtype=jnp.float32) / np.sqrt(D_in)
        gate_w = jax.random.normal(ks[2], (E, D_in), dtype=jnp.float32) / np.sqrt(D_in)
        lora_U = jax.random.normal(ks[3], (E, R, D_in), dtype=jnp.float32) / np.sqrt(D_in)
        lora_V = jax.random.normal(ks[4], (E, D_out, R), dtype=jnp.float32) / np.sqrt(R)
        return {'x': x, 'weight': weight, 'gate_w': gate_w, 'lora_U': lora_U, 'lora_V': lora_V}
    _L0_ffn_in = _L0_ffn_setup()
    _d = {'L0_attn_x': _L0_attn_in['x'], 'L0_attn_wq': _L0_attn_in['wq'], 'L0_attn_wk': _L0_attn_in['wk'], 'L0_attn_wv': _L0_attn_in['wv'], 'L0_attn_wo': _L0_attn_in['wo'], 'L0_attn_q_norm_w': _L0_attn_in['q_norm_w'], 'L0_attn_k_norm_w': _L0_attn_in['k_norm_w'], 'L0_ffn_weight': _L0_ffn_in['weight'], 'L0_ffn_gate_w': _L0_ffn_in['gate_w'], 'L0_ffn_lora_U': _L0_ffn_in['lora_U'], 'L0_ffn_lora_V': _L0_ffn_in['lora_V']}
    _x0 = _d['L0_attn_x']
    _d['L0_attn_x'] = jax.random.normal(jax.random.fold_in(jax.random.key(seed), 1), (32, 512, 256), dtype=_x0.dtype)
    del _x0
    return _d

def reference(L0_attn_x, L0_attn_wq, L0_attn_wk, L0_attn_wv, L0_attn_wo, L0_attn_q_norm_w, L0_attn_k_norm_w, L0_ffn_weight, L0_ffn_gate_w, L0_ffn_lora_U, L0_ffn_lora_V):

    def _L0_attn_ref(x, wq, wk, wv, wo, q_norm_w, k_norm_w):
        import jax, jax.numpy as jnp
        import numpy as np
        DIM, H, KV, HD, WIN = (256, 16, 4, 64, 128)
        EPS = 1e-06

        def rmsnorm(x, w, eps=EPS):
            return x * jax.lax.rsqrt(jnp.mean(x * x, axis=-1, keepdims=True) + eps) * w
        B, T, D = x.shape
        rep = H // KV
        q = (x @ wq.T).reshape(B, T, H, HD)
        k = (x @ wk.T).reshape(B, T, KV, HD)
        v = (x @ wv.T).reshape(B, T, KV, HD)
        q = rmsnorm(q, q_norm_w)
        k = rmsnorm(k, k_norm_w)
        k = jnp.repeat(k, rep, axis=2)
        v = jnp.repeat(v, rep, axis=2)
        scores = jnp.einsum('bqhd,bkhd->bhqk', q, k) / jnp.sqrt(jnp.float32(HD))
        i = jnp.arange(T)[:, None]
        j = jnp.arange(T)[None, :]
        mask = (i >= j) & (i - j < WIN)
        scores = jnp.where(mask, scores, -jnp.inf)
        attn = jax.nn.softmax(scores, axis=-1)
        y = jnp.einsum('bhqk,bkhd->bqhd', attn, v).reshape(B, T, H * HD)
        return y @ wo.T

    def _L0_ffn_ref(x, weight, gate_w, lora_U, lora_V):
        import jax, jax.numpy as jnp
        import numpy as np
        scaling = 1.0 / lora_U.shape[1]
        B, S, D_in = x.shape
        xt = x.reshape(-1, D_in)
        gate = jax.nn.softmax(xt @ gate_w.T, axis=-1)
        base = xt @ weight.T
        t = jnp.einsum('nh,erh->ner', xt, lora_U)
        lora = jnp.einsum('ne,eor,ner->no', gate, lora_V, t)
        out = base + scaling * lora
        return out.reshape(B, S, -1)
    x = L0_attn_x
    x = x + _L0_attn_ref(_layernorm(x, axis=-1), L0_attn_wq, L0_attn_wk, L0_attn_wv, L0_attn_wo, L0_attn_q_norm_w, L0_attn_k_norm_w)
    x = x + _L0_ffn_ref(_layernorm(x, axis=-1), L0_ffn_weight, L0_ffn_gate_w, L0_ffn_lora_U, L0_ffn_lora_V)
    return x

_drawn_inputs = setup_inputs


def setup_inputs(seed=0):
    import zlib

    import numpy as np

    out = dict(_drawn_inputs(seed))
    spreads = {'L0_attn_q_norm_w': (1.0, 0.6), 'L0_attn_k_norm_w': (1.0, 0.6)}
    factors = {'L0_ffn_gate_w': 3.823}
    for name, (base, spread) in spreads.items():
        noise = np.random.default_rng([zlib.crc32(name.encode()), seed]).standard_normal(out[name].shape)
        drawn = base * np.exp(spread * noise) if base else spread * noise
        out[name] = jnp.asarray(drawn.astype(out[name].dtype))
    for name, factor in factors.items():
        out[name] = (out[name] * factor).astype(out[name].dtype)
    return out
```

```python
import concourse.bass as bass
from concourse import mybir
from contextlib import ExitStack

F32 = mybir.dt.float32
F32R = mybir.dt.float32r
I32 = mybir.dt.int32
ALU = mybir.AluOpType
ACT = mybir.ActivationFunctionType
AX = mybir.AxisListType

P = 128
SEQS, SEQ_LEN, DIM = 32, 512, 256
HEADS, KV_HEADS, HD = 16, 4, 64
REP = HEADS // KV_HEADS
QDIM, KVDIM = HEADS * HD, KV_HEADS * HD
EXPERTS, RANK = 8, 16
ER = EXPERTS * RANK
FFN_OUT = DIM + ER + EXPERTS
KC = DIM // P
YC = QDIM // P
TPS = SEQ_LEN // P
TILES = SEQS * TPS
BANK = 512
LN_EPS, RMS_EPS = 1e-5, 1e-6
MASKED = -1e30
CONSTANTS = 7


class Tile:

    def __init__(self, j, k):
        self.j, self.k = j, k

    def __add__(self, d):
        return Tile(self.j, self.k + d)

    def __sub__(self, d):
        return Tile(self.j, self.k - d)

    @property
    def live(self):
        return not isinstance(self.j, int) or 0 <= TPS * self.j + self.k < TILES

    @property
    def slot(self):
        return self.k % TPS

    @property
    def par(self):
        return self.k % 2

    def count(self, per=1, more=0):
        return self.j * (TPS * per) + (self.k * per + more)

    def turn(self, ring):
        return self.j * (TPS // ring) + (self.k // ring + 1)


class Group:

    def __init__(self, tile, g):
        self.tile, self.g = tile + g // KV_HEADS, g % KV_HEADS

    @property
    def live(self):
        return self.tile.live

    @property
    def par(self):
        return self.g % 2

    def done(self, before=0):
        return self.tile.count(KV_HEADS, self.g + 1 - before)

    def prev_done(self):
        n, k = KV_HEADS * (TPS - 1), self.tile.k
        return self.tile.j * n + (k // TPS * n + (KV_HEADS * (k % TPS - 1) + self.g + 1 if k % TPS else 0))


def wait(eng, sem, value):
    if not isinstance(value, int) or value > 0:
        eng.wait_ge(sem, value)


def steps(eng, step):
    for T in range(-2, 1):
        step(Tile(0, T))
    with eng.Fori(0, TILES // TPS - 1) as j:
        for k in range(1, TPS + 1):
            step(Tile(j, k))
    for T in range(TILES - TPS + 1, TILES + 1):
        step(Tile(0, T))


def layer(nc, x, w_qkv, w_o, w_ffn, w_v, norm_w, out):
    ctx = ExitStack()
    with ctx:
        def sb(name, shape, dt=F32):
            return ctx.enter_context(nc.sbuf_tensor(name, shape, dt))

        def sem(name):
            return ctx.enter_context(nc.semaphore(name))

        wqkv_h, wqkv_l = (sb(f"wqkv_{n}", [P, KC, QDIM + 2 * KVDIM], F32R) for n in "hl")
        wo_h, wo_l = (sb(f"wo_{n}", [P, YC, DIM], F32R) for n in "hl")
        wffn_h, wffn_l = (sb(f"wffn_{n}", [P, KC, FFN_OUT], F32R) for n in "hl")
        wv_h, wv_l = (sb(f"wv_{n}", [P, 1, DIM], F32R) for n in "hl")
        w_plain = sb("w_plain", [P, KC * (QDIM + 2 * KVDIM)])
        nw = sb("nw", [P, 2])
        qk_w = sb("qk_w", [P, 1])
        ident, ident_r = sb("ident", [P, P]), sb("ident_r", [P, P], F32R)
        later_key = sb("later_key", [P, P])
        neg_later = sb("neg_later", [P, P])
        minus_half = sb("minus_half", [P, HEADS])
        pool_spare = sb("pool_spare", [P, KV_HEADS])
        xs = sb("xs", [P, TPS, DIM])
        x_stats, x_mv, x_ve, x_rstd = sb("x_stats", [P, 6]), sb("x_mv", [P, 2]), sb("x_ve", [P, 1]), sb("x_rstd", [P, 1])
        xn = sb("xn", [P, DIM])
        xT_h, xT_l = sb("xT_h", [P, KC, P], F32R), sb("xT_l", [P, KC, P], F32R)
        k_sq, k_ms, k_ve, k_r = sb("k_sq", [P, KVDIM]), sb("k_ms", [P, KV_HEADS]), sb("k_ve", [P, KV_HEADS]), sb("k_r", [P, KV_HEADS])
        q_sq = [sb(f"q_sq{n}", [P, BANK]) for n in range(2)]
        q_ms, q_ve, q_r = sb("q_ms", [P, HEADS]), sb("q_ve", [P, HEADS]), sb("q_r", [P, HEADS])
        k_nn = sb("k_nn", [P, KV_HEADS, 2, HD])
        q_n = sb("q_n", [P, HEADS, HD])
        q_hl = sb("q_hl", [P, HEADS, 2, HD], F32R)
        qT = sb("qT", [P, 2, HEADS, P], F32R)
        kT_h, kT_l = (sb(n, [P, KV_HEADS, (TPS + 1) * P], F32R) for n in ("kT_h", "kT_l"))
        vz_h, vz_l = (sb(n, [P, TPS, KV_HEADS, 3 * HD], F32R) for n in ("vz_h", "vz_l"))
        merged = sb("merged", [P, 2, REP, P])
        neg_max, den, rden = sb("neg_max", [P, 2, REP]), sb("den", [P, 2, REP]), sb("rden", [P, 2, REP])
        probs = sb("probs", [P, 2, REP, P])
        pT = sb("pT", [P, 2, 2, REP, P], F32R)
        pT_own, pT_prev = (sb(n, [P, 2, 2, REP, P], F32R) for n in ("pT_own", "pT_prev"))
        yT_h, yT_l = sb("yT_h", [P, YC, P], F32R), sb("yT_l", [P, YC, P], F32R)
        x1, hn = sb("x1", [P, DIM]), sb("hn", [P, DIM])
        h_stats, h_mv, h_ve, h_rstd = sb("h_stats", [P, 6]), sb("h_mv", [P, 2]), sb("h_ve", [P, 1]), sb("h_rstd", [P, 1])
        hT_h, hT_l = sb("hT_h", [P, KC, P], F32R), sb("hT_l", [P, KC, P], F32R)
        g_negmax, g_exp, g_den, g_rden, gate = sb("g_negmax", [P, 1]), sb("g_exp", [P, EXPERTS]), sb("g_den", [P, 1]), sb("g_rden", [P, 1]), sb("gate", [P, EXPERTS])
        tg = sb("tg", [P, EXPERTS, RANK])
        tgT_h, tgT_l = sb("tgT_h", [P, P], F32R), sb("tgT_l", [P, P], F32R)
        ob = sb("ob", [P, 2, DIM])

        ps_scores = ctx.enter_context(nc.psum_tensor("ps_scores", [P, REP, 2 * P], F32))
        ps_pT = ctx.enter_context(nc.psum_tensor("ps_pT", [P, REP, P], F32))
        ps_y = ctx.enter_context(nc.psum_tensor("ps_y", [P, BANK], F32))
        ps_post = ctx.enter_context(nc.psum_tensor("ps_post", [P, BANK], F32))
        ps_a, ps_b, ps_c = (ctx.enter_context(nc.psum_tensor(f"ps_{n}", [P, BANK], F32)) for n in "abc")

        s_w, s_nwl = sem("weights_loaded"), sem("norm_weights_loaded")
        s_wh, s_wl, s_const, s_ident_r, s_zero, s_nw = (sem(n) for n in ("weights_high", "weights_low", "constants_set", "ident_r_set", "zeros_set", "norm_product_set"))
        s_x = [sem(f"x_loaded{n}") for n in range(TPS)]
        s_xst, s_xmv, s_xve, s_xrstd, s_xn, s_xt, s_xth, s_xtl = (sem(n) for n in ("x_stats_done", "x_mean_done", "x_var_done", "x_rstd_done", "x_normed", "x_transposed", "xT_high", "xT_low"))
        s_kv, s_q = sem("kv_projected"), [sem(f"q{n}_projected") for n in range(2)]
        s_ksq, s_kms, s_kve, s_kr, s_kn = (sem(n) for n in ("k_squared", "k_summed", "k_mean_square", "k_rms_done", "k_normed"))
        s_vh, s_vl = sem("v_high"), sem("v_low")
        s_qsq, s_qms, s_qve, s_qr, s_qn, s_qh, s_ql = ([sem(f"q{n}_{what}") for n in range(2)] for what in ("squared", "summed", "mean_square", "rms_done", "normed", "high", "low"))
        s_kt, s_kth, s_ktl = sem("k_transposed"), sem("kT_high"), sem("kT_low")
        s_qt, s_qT = sem("q_transposed"), sem("qT_stored")
        s_s, s_own, s_merged, s_max, s_exp, s_rden, s_pn = (sem(n) for n in ("scores_done", "own_scores_copied", "scores_merged", "max_done", "exp_done", "rden_done", "probs_normed"))
        s_pt, s_ph, s_pl, s_po, s_pp, s_pv, s_yh, s_yl = (sem(n) for n in ("probs_transposed", "pT_high", "pT_low", "pT_own_done", "pT_prev_done", "pv_done", "yT_high", "yT_low"))
        s_o, s_x1, s_hst, s_hmv, s_hve, s_hrstd, s_hn, s_ht, s_hth, s_htl = (sem(n) for n in ("o_projected", "x1_done", "h_stats_done", "h_mean_done", "h_var_done", "h_rstd_done", "h_normed", "h_transposed", "hT_high", "hT_low"))
        s_ffn, s_gmax, s_gexp, s_grd, s_gate, s_tg, s_tt, s_tth, s_ttl, s_lv = (sem(n) for n in ("ffn_projected", "gate_max_done", "gate_exp_done", "gate_rden_done", "gate_done", "t_gated", "t_transposed", "tgT_high", "tgT_low", "lora_added"))
        s_ob = sem("out_ready")
        s_st = [sem(f"out_stored{n}") for n in range(2)]

        block = ctx.enter_context(nc.Block())
        WEIGHTS = [(w_qkv, wqkv_h, wqkv_l), (w_ffn, wffn_h, wffn_l), (w_o, wo_h, wo_l), (w_v, wv_h, wv_l)]

        def plain(h):
            _, c, n = h.shape
            return w_plain[:, 0:c * n].rearrange("p (c n) -> p c n", c=c)

        @block.sync
        def _(sp):
            def load_x(tile):
                sp.dma_start(xs[:, tile.slot, :], x[bass.ds(tile.count(P), P), :]).then_inc(s_x[tile.slot], 16)

            load_x(Tile(0, 0))
            sp.dma_start(nw[:], norm_w).then_inc(s_nwl, 16)
            for n, (w, h, _low) in enumerate(WEIGHTS):
                if n:
                    sp.wait_ge(s_wl, n)
                sp.dma_start(plain(h), w.rearrange("(c p) n -> p c n", p=P)).then_inc(s_w, 16)
            load_x(Tile(0, 1))
            load_x(Tile(0, 2))

            def step(T):
                if (T + 3).live and T.k >= 0:
                    wait(sp, s_x1, T.count())
                    load_x(T + 3)
                if (T - 1).live:
                    sp.wait_ge(s_ob, T.count())
                    sp.dma_start(out[bass.ds((T - 1).count(P), P), :], ob[:, (T - 1).par, :]).then_inc(s_st[(T - 1).par], 16)

            steps(sp, step)
            for n in range(2):
                sp.wait_ge(s_st[n], 16 * (TILES // 2))

        @block.gpsimd
        def _(pool):
            pool.memset(ident[:], 0.0).then_inc(s_const, 1)
            pool.memset(later_key[:], 0.0).then_inc(s_const, 1)
            pool.memset(neg_later[:], 0.0).then_inc(s_const, 1)
            pool.memset(minus_half[:], -0.5).then_inc(s_const, 1)
            pool.wait_ge(s_const, 4)
            pool.affine_select(out=ident[:], in_=ident[:], compare_op=ALU.not_equal, fill=1.0, base=0,
                               pattern=[[-1, P]], channel_multiplier=1).then_inc(s_const, 1)
            for m, fill in ((later_key, 1.0), (neg_later, MASKED)):
                pool.affine_select(out=m[:], in_=m[:], compare_op=ALU.is_ge, fill=fill, base=0,
                                   pattern=[[-1, P]], channel_multiplier=1).then_inc(s_const, 1)

            def split_probs(G):
                if not G.live:
                    return
                b = G.par
                src = pT[:, b].bitcast(F32).rearrange("p a h q -> p (a h) q")
                wait(pool, s_pl, G.done())
                wait(pool, s_pv, G.done(2))
                pool.tensor_tensor(pool_spare[:, G.g:G.g + 1], minus_half[:, 0:1], minus_half[:, 0:1], ALU.mult)
                pool.affine_select(out=pT_own[:, b].rearrange("p a h q -> p (a h) q"), in_=src, compare_op=ALU.is_ge,
                                   fill=0.0, base=0, pattern=[[0, 2 * REP], [1, P]], channel_multiplier=-1).then_inc(s_po, 1)
                if G.tile.slot:
                    pool.affine_select(out=pT_prev[:, b].rearrange("p a h q -> p (a h) q"), in_=src, compare_op=ALU.is_gt,
                                       fill=0.0, base=0, pattern=[[0, 2 * REP], [-1, P]], channel_multiplier=1).then_inc(s_pp, 1)

            def power(tile, ready, out_, in_, done):
                if tile.live:
                    pool.wait_ge(ready, (tile + 1).count())
                    n = in_.shape[-1]
                    pool.tensor_tensor(out_, in_, minus_half[:, 0:n], ALU.pow).then_inc(done, 1)

            def step(T):
                split_probs(Group(T, 0))
                power(T + 1, s_qve[1], q_r[:, 8:16], q_ve[:, 8:16], s_qr[1])
                split_probs(Group(T, 1))
                power(T - 1, s_hve, h_rstd[:], h_ve[:], s_hrstd)
                power(T + 2, s_xve, x_rstd[:], x_ve[:], s_xrstd)
                split_probs(Group(T, 2))
                split_probs(Group(T, 3))
                power(T + 2, s_kve, k_r[:], k_ve[:], s_kr)
                power(T + 2, s_qve[0], q_r[:, 0:8], q_ve[:, 0:8], s_qr[0])

            steps(pool, step)

        @block.scalar
        def _(act):
            for n, (_w, h, _low) in enumerate(WEIGHTS):
                act.wait_ge(s_w, 16 * (n + 1))
                nc.scalar.activation(h[:], plain(h), ACT.Copy).then_inc(s_wh, 1)

            def high_probs(G):
                if G.live:
                    act.wait_ge(s_pt, G.done())
                    wait(act, s_po, G.done(2))
                    wait(act, s_pp, Group(G.tile, G.g - 2).prev_done())
                    nc.scalar.activation(pT[:, G.par, 0], ps_pT[:], ACT.Copy).then_inc(s_ph, 1)

            def exps(G):
                if G.live:
                    act.wait_ge(s_max, G.done())
                    wait(act, s_pt, G.done(2))
                    for h in range(REP):
                        last = nc.scalar.activation(probs[:, G.par, h], merged[:, G.par, h], ACT.Exp,
                                                    bias=neg_max[:, G.par, h:h + 1], accum_out=den[:, G.par, h:h + 1])
                    last.then_inc(s_exp, 1)

            def own_scores(G):
                if G.live and G.tile.slot:
                    act.wait_ge(s_s, G.done())
                    wait(act, s_exp, G.done(2))
                    nc.scalar.activation(merged[:, G.par], ps_scores[:, :, P:2 * P], ACT.Copy).then_inc(s_own, 1)

            def high_y(G):
                if G.live:
                    act.wait_ge(s_pv, G.done())
                    nc.scalar.activation(yT_h[:, 2 * G.g:2 * G.g + 2], ps_y[:, 0:2 * P].rearrange("p (c q) -> p c q", c=2), ACT.Copy).then_inc(s_yh, 1)

            def square_q(tile, n, ps):
                if tile.live:
                    act.wait_ge(s_q[n], (tile + 1).count())
                    nc.scalar.activation(q_sq[n][:], ps[:], ACT.Square).then_inc(s_qsq[n], 1)

            def store_qT(tile, n, ps):
                if tile.live:
                    act.wait_ge(s_qt, tile.count(4, n + 1))
                    nc.scalar.activation(qT[:, tile.par, 4 * n:4 * n + 4], ps[:].rearrange("p (h q) -> p h q", h=4), ACT.Copy).then_inc(s_qT, 1)

            def high_T(tile, ready, out_, ps, n, done):
                if tile.live:
                    act.wait_ge(ready, (tile + 1).count())
                    nc.scalar.activation(out_, ps[:, 0:n], ACT.Copy).then_inc(done, 1)

            def step(T):
                high_probs(Group(T, 0))
                exps(Group(T, 1))
                own_scores(Group(T, 2))
                square_q(T + 1, 1, ps_b)
                high_y(Group(T - 1, 3))
                high_probs(Group(T, 1))
                exps(Group(T, 2))
                own_scores(Group(T, 3))
                if (T + 1).live:
                    act.wait_ge(s_kt, (T + 2).count())
                    if T.k == -1:
                        act.wait_ge(s_nw, 1)
                    c = ((T + 1).slot + 1) * P
                    nc.scalar.activation(kT_h[:, :, c:c + P], ps_c[:].rearrange("p (g k) -> p g k", g=KV_HEADS), ACT.Copy,
                                         scale=qk_w[:, 0:1]).then_inc(s_kth, 1)
                store_qT(T + 1, 0, ps_a)
                store_qT(T + 1, 1, ps_b)
                high_y(Group(T, 0))
                high_probs(Group(T, 2))
                exps(Group(T, 3))
                own_scores(Group(T + 1, 0))
                store_qT(T + 1, 2, ps_a)
                store_qT(T + 1, 3, ps_b)
                high_T(T - 1, s_ht, hT_h[:].rearrange("p c q -> p (c q)"), ps_c, DIM, s_hth)
                high_T(T + 2, s_xt, xT_h[:].rearrange("p c q -> p (c q)"), ps_c, DIM, s_xth)
                high_y(Group(T, 1))
                high_probs(Group(T, 3))
                exps(Group(T + 1, 0))
                own_scores(Group(T + 1, 1))
                if (T - 1).live:
                    act.wait_ge(s_gmax, T.count())
                    nc.scalar.activation(g_exp[:], ps_post[:, DIM + ER:FFN_OUT], ACT.Exp, bias=g_negmax[:, 0:1],
                                         accum_out=g_den[:, 0:1]).then_inc(s_gexp, 1)
                high_T(T - 1, s_tt, tgT_h[:], ps_b, P, s_tth)
                if (T + 2).live:
                    act.wait_ge(s_kv, (T + 3).count())
                    nc.scalar.activation(k_sq[:], ps_c[:, 0:KVDIM], ACT.Square).then_inc(s_ksq, 1)
                    if T.k == -2:
                        act.wait_ge(s_zero, 1)
                    nc.scalar.activation(vz_h[:, (T + 2).slot, :, HD:2 * HD], ps_c[:, KVDIM:].rearrange("p (g d) -> p g d", g=KV_HEADS),
                                         ACT.Copy).then_inc(s_vh, 1)
                square_q(T + 2, 0, ps_a)
                high_y(Group(T, 2))

            steps(act, step)

        @block.vector
        def _(dve):
            dve.wait_ge(s_const, CONSTANTS)
            nc.vector.tensor_copy(ident_r[:], ident[:]).then_inc(s_ident_r, 1)
            for m in (vz_h, vz_l):
                for s in range(TPS):
                    last = nc.vector.memset(m[:, s].bitcast(F32), 0.0)
            for m in (kT_h, kT_l):
                last = nc.vector.memset(m[:, :, 0:P].bitcast(F32), 0.0)
            last.then_inc(s_zero, 1)
            dve.wait_ge(s_nwl, 16)
            nc.vector.tensor_scalar(qk_w[:], nw[:, 0:1], nw[:, 1:2], float(HD) ** -0.5, ALU.mult, ALU.mult).then_inc(s_nw, 1)
            for n, (_w, h, low) in enumerate(WEIGHTS):
                dve.wait_ge(s_wh, n + 1)
                nc.vector.tensor_tensor(low[:], plain(h), h[:].bitcast(F32), ALU.subtract).then_inc(s_wl, 1)

            def mean_and_var(tile, st, mv, ve, s_st_, s_mv_, s_ve_):
                n = (tile + 1).count()
                if isinstance(n, int):
                    dve.wait_ge(s_st_, n)
                nc.vector.bn_aggr(mv[:], st[:]).then_inc(s_mv_, 1)
                dve.wait_ge(s_mv_, n)
                nc.vector.tensor_scalar_add(ve[:], mv[:, 1:2], LN_EPS).then_inc(s_ve_, 1)

            def low_probs(G):
                if G.live:
                    dve.wait_ge(s_ph, G.done())
                    nc.vector.tensor_tensor(pT[:, G.par, 1], ps_pT[:], pT[:, G.par, 0].bitcast(F32), ALU.subtract).then_inc(s_pl, 1)

            def merge_and_norm(new, old):
                if new.live and new.tile.slot:
                    dve.wait_ge(s_own, new.prev_done())
                if old.live:
                    dve.wait_ge(s_exp, old.done())
                    nc.vector.reciprocal(rden[:, old.par], den[:, old.par]).then_inc(s_rden, 1)
                if new.live:
                    m = merged[:, new.par]
                    every = [P, REP, P]
                    if new.tile.slot:
                        nc.vector.copy_predicated(m, later_key[:].bitcast(I32).unsqueeze(1).to_broadcast(every),
                                                  ps_scores[:, :, 0:P]).then_inc(s_merged, 1)
                    else:
                        dve.wait_ge(s_s, new.done())
                        wait(dve, s_exp, new.done(2))
                        nc.vector.tensor_tensor(m, ps_scores[:, :, P:2 * P], neg_later[:].unsqueeze(1).to_broadcast(every),
                                                ALU.add).then_inc(s_merged, 1)
                    dve.wait_ge(s_merged, new.done())
                    nc.vector.tensor_reduce(neg_max[:, new.par], m, AX.X, ALU.max, negate=True).then_inc(s_max, 1)
                if old.live:
                    dve.wait_ge(s_rden, old.done())
                    nc.vector.tensor_tensor(probs[:, old.par], probs[:, old.par], rden[:, old.par].unsqueeze(2).to_broadcast([P, REP, P]),
                                            ALU.mult).then_inc(s_pn, 1)

            def low_y(G):
                if G.live:
                    dve.wait_ge(s_yh, G.done())
                    c = slice(2 * G.g, 2 * G.g + 2)
                    nc.vector.tensor_tensor(yT_l[:, c], ps_y[:, 0:2 * P].rearrange("p (c q) -> p c q", c=2), yT_h[:, c].bitcast(F32),
                                            ALU.subtract).then_inc(s_yl, 1)

            def mean_square(tile, sq, ms, ve, ready, s1, s2):
                if tile.live:
                    n = (tile + 1).count()
                    dve.wait_ge(ready, n)
                    nc.vector.reduce_sum(ms, sq.rearrange("p (h d) -> p h d", d=HD), AX.X).then_inc(s1, 1)
                    dve.wait_ge(s1, n)
                    nc.vector.tensor_scalar(ve, ms, 1.0 / HD, RMS_EPS, ALU.mult, ALU.add).then_inc(s2, 1)

            def norm_q(tile, n, ps):
                if not tile.live:
                    return
                c, every = slice(8 * n, 8 * n + 8), [P, 8, HD]
                done = (tile + 1).count()
                dve.wait_ge(s_qr[n], done)
                nc.vector.tensor_tensor(q_n[:, c], ps[:].rearrange("p (h d) -> p h d", d=HD), q_r[:, c].unsqueeze(2).to_broadcast(every),
                                        ALU.mult).then_inc(s_qn[n], 1)
                dve.wait_ge(s_qn[n], done)
                wait(dve, s_qt, tile.count(4, 2 * n + 2 - 4))
                nc.vector.tensor_copy(q_hl[:, c, 0], q_n[:, c]).then_inc(s_qh[n], 1)
                dve.wait_ge(s_qh[n], done)
                nc.vector.tensor_tensor(q_hl[:, c, 1], q_n[:, c], q_hl[:, c, 0].bitcast(F32), ALU.subtract).then_inc(s_ql[n], 1)

            def low_T(tile, ready, out_, ps, n, hi, done):
                if tile.live:
                    dve.wait_ge(ready, (tile + 1).count())
                    nc.vector.tensor_tensor(out_, ps[:, 0:n], hi.bitcast(F32), ALU.subtract).then_inc(done, 1)

            def flat(a):
                return a[:].rearrange("p c q -> p (c q)")

            def step(T):
                low_probs(Group(T, 0))
                merge_and_norm(Group(T, 2), Group(T, 1))
                norm_q(T + 1, 0, ps_a)
                mean_square(T + 1, q_sq[1][:], q_ms[:, 8:16], q_ve[:, 8:16], s_qsq[1], s_qms[1], s_qve[1])
                low_y(Group(T - 1, 3))
                low_probs(Group(T, 1))
                merge_and_norm(Group(T, 3), Group(T, 2))
                if (T - 1).live:
                    dve.wait_ge(s_o, T.count())
                    nc.vector.tensor_tensor(x1[:], ps_post[:, 0:DIM], xs[:, (T - 1).slot], ALU.add).then_inc(s_x1, 1)
                    dve.wait_ge(s_x1, T.count())
                    nc.vector.bn_stats(h_stats[:], x1[:]).then_inc(s_hst, 1)
                    dve.wait_ge(s_hst, T.count())
                norm_q(T + 1, 1, ps_b)
                if (T - 1).live:
                    mean_and_var(T - 1, h_stats, h_mv, h_ve, s_hst, s_hmv, s_hve)
                if (T + 2).live:
                    dve.wait_ge(s_x[(T + 2).slot], (T + 2).turn(TPS) * 16)
                    nc.vector.bn_stats(x_stats[:], xs[:, (T + 2).slot]).then_inc(s_xst, 1)
                    dve.wait_ge(s_xst, (T + 3).count())
                if (T + 1).live:
                    dve.wait_ge(s_kth, (T + 2).count())
                    c = ((T + 1).slot + 1) * P
                    nc.vector.scalar_tensor_tensor(kT_l[:, :, c:c + P], ps_c[:].rearrange("p (g k) -> p g k", g=KV_HEADS), qk_w[:, 0:1],
                                                   kT_h[:, :, c:c + P].bitcast(F32), op0=ALU.mult, op1=ALU.subtract).then_inc(s_ktl, 1)
                if (T + 2).live:
                    mean_and_var(T + 2, x_stats, x_mv, x_ve, s_xst, s_xmv, s_xve)
                if (T - 1).live:
                    dve.wait_ge(s_hrstd, T.count())
                    nc.vector.tensor_scalar(hn[:], x1[:], h_mv[:, 0:1], h_rstd[:, 0:1], ALU.subtract, ALU.mult).then_inc(s_hn, 1)
                low_y(Group(T, 0))
                low_probs(Group(T, 2))
                if (T + 2).live:
                    dve.wait_ge(s_xrstd, (T + 3).count())
                    nc.vector.tensor_scalar(xn[:], xs[:, (T + 2).slot], x_mv[:, 0:1], x_rstd[:, 0:1], ALU.subtract, ALU.mult).then_inc(s_xn, 1)
                merge_and_norm(Group(T + 1, 0), Group(T, 3))
                low_T(T - 1, s_hth, flat(hT_l), ps_c, DIM, flat(hT_h), s_htl)
                low_T(T + 2, s_xth, flat(xT_l), ps_c, DIM, flat(xT_h), s_xtl)
                low_y(Group(T, 1))
                low_probs(Group(T, 3))
                merge_and_norm(Group(T + 1, 1), Group(T + 1, 0))
                if (T - 1).live:
                    dve.wait_ge(s_ffn, T.count())
                    nc.vector.tensor_reduce(g_negmax[:], ps_post[:, DIM + ER:FFN_OUT], AX.X, ALU.max, negate=True).then_inc(s_gmax, 1)
                if (T - 1).live:
                    dve.wait_ge(s_gexp, T.count())
                    nc.vector.reciprocal(g_rden[:], g_den[:]).then_inc(s_grd, 1)
                    dve.wait_ge(s_grd, T.count())
                    nc.vector.tensor_scalar(gate[:], g_exp[:], g_rden[:, 0:1], 1.0 / RANK, ALU.mult, ALU.mult).then_inc(s_gate, 1)
                    dve.wait_ge(s_gate, T.count())
                    nc.vector.tensor_tensor(tg[:], ps_post[:, DIM:DIM + ER].rearrange("p (e r) -> p e r", e=EXPERTS),
                                            gate[:].unsqueeze(2).to_broadcast([P, EXPERTS, RANK]), ALU.mult).then_inc(s_tg, 1)
                mean_square(T + 2, k_sq[:], k_ms[:], k_ve[:], s_ksq, s_kms, s_kve)
                low_T(T - 1, s_tth, tgT_l[:], ps_b, P, tgT_h[:], s_ttl)
                if (T + 2).live:
                    dve.wait_ge(s_vh, (T + 3).count())
                    s = (T + 2).slot
                    nc.vector.tensor_tensor(vz_l[:, s, :, HD:2 * HD], ps_c[:, KVDIM:].rearrange("p (g d) -> p g d", g=KV_HEADS),
                                            vz_h[:, s, :, HD:2 * HD].bitcast(F32), ALU.subtract).then_inc(s_vl, 1)
                    dve.wait_ge(s_kr, (T + 3).count())
                    wait(dve, s_kt, (T + 2).count())
                    every = [P, KV_HEADS, 2, HD]
                    nc.vector.tensor_tensor(k_nn[:], ps_c[:, 0:KVDIM].rearrange("p (g d) -> p g d", g=KV_HEADS).unsqueeze(2).to_broadcast(every),
                                            k_r[:].unsqueeze(2).unsqueeze(3).to_broadcast(every), ALU.mult).then_inc(s_kn, 1)
                mean_square(T + 2, q_sq[0][:], q_ms[:, 0:8], q_ve[:, 0:8], s_qsq[0], s_qms[0], s_qve[0])
                if (T - 1).live:
                    dve.wait_ge(s_lv, T.count())
                    wait(dve, s_st[(T - 1).par], (T - 1).turn(2) * 16 - 16)
                    nc.vector.tensor_tensor(ob[:, (T - 1).par], ps_post[:, 0:DIM], x1[:], ALU.add).then_inc(s_ob, 1)
                low_y(Group(T, 2))

            steps(dve, step)

        @block.tensor
        def _(pe):
            def three(ps, stat_h, stat_l, mov_h, mov_l, first, last, onto_ended=False):
                nc.tensor.matmul(ps, stat_h, mov_h, start=first, stop=False, skip_group_check=onto_ended)
                nc.tensor.matmul(ps, stat_l, mov_h, start=False, stop=False, skip_group_check=onto_ended)
                return nc.tensor.matmul(ps, stat_h, mov_l, start=False, stop=last, skip_group_check=onto_ended)

            def transpose_probs(G):
                if G.live:
                    pe.wait_ge(s_pn, G.done())
                    wait(pe, s_pl, G.done(1))
                    for h in range(REP):
                        last = nc.tensor.transpose(ps_pT[:, h], probs[:, G.par, h], ident[:])
                    last.then_inc(s_pt, 1)

            def scores(G):
                if not G.live:
                    return
                T, g = G.tile, G.g
                pe.wait_ge(s_qT, T.count(4, g + 1))
                if g == 0:
                    pe.wait_ge(s_ktl, (T + 1).count())
                wait(pe, s_merged, G.done(1))
                keys = slice(T.slot * P, (T.slot + 2) * P)
                for h in range(REP):
                    q = qT[:, T.par, REP * g + h]
                    nc.tensor.matmul(ps_scores[:, h], q, kT_h[:, g, keys], start=True, stop=False)
                    last = nc.tensor.matmul(ps_scores[:, h], q, kT_l[:, g, keys], start=False, stop=True)
                last.then_inc(s_s, 1)

            def attend(G):
                if not G.live:
                    return
                T, g = G.tile, G.g
                wait(pe, s_yl, G.done(1))
                blocks = [(T.slot, pT_own)] + ([(T.slot - 1, pT_prev)] if T.slot else [])
                pe.wait_ge(s_po, G.done())
                if g == 0:
                    pe.wait_ge(s_vl, (T + 1).count())
                n = 0
                for s, pt in blocks:
                    if n:
                        pe.wait_ge(s_pp, G.prev_done())
                    for half in range(2):
                        cols = slice(HD - HD * half, HD - HD * half + P)
                        vh, vl = vz_h[:, s, g, cols], vz_l[:, s, g, cols]
                        ph, pl = (pt[:, G.par, m, 2 * half:2 * half + 2] for m in range(2))
                        for v, p in ((vh, ph), (vl, ph), (vh, pl)):
                            last = nc.tensor.matmul(ps_y[:, 0:2 * P], v, p, start=n == 0, stop=n == 6 * len(blocks) - 1)
                            n += 1
                last.then_inc(s_pv, 1)

            def project(tile, ps, cols, done):
                for c in range(KC):
                    last = three(ps[:, 0:cols.stop - cols.start], xT_h[:, c], xT_l[:, c], wqkv_h[:, c, cols], wqkv_l[:, c, cols], c == 0, c == KC - 1)
                last.then_inc(done, 1)

            def out_project(tile, chunks):
                for c in chunks:
                    last = three(ps_post[:, 0:DIM], yT_h[:, c], yT_l[:, c], wo_h[:, c], wo_l[:, c], c == 0, c == YC - 1)
                return last

            def transpose_q(tile, n, ps):
                if tile.live:
                    for h in range(4):
                        last = nc.tensor.transpose(ps[:, h * P:(h + 1) * P].bitcast(F32R), q_hl[:, 4 * n + h].rearrange("p a d -> p (a d)"), ident_r[:])
                    last.then_inc(s_qt, 1)

            pe.wait_ge(s_const, CONSTANTS)
            pe.wait_ge(s_ident_r, 1)
            pe.wait_ge(s_zero, 1)
            pe.wait_ge(s_wl, 1)

            def step(T):
                transpose_probs(Group(T, 0))
                scores(Group(T, 2))
                if (T - 1).live:
                    pe.wait_ge(s_yl, T.count(4, -1))
                    wait(pe, s_ob, (T - 1).count())
                    out_project(T - 1, range(0, YC - 2))
                if (T + 1).live:
                    wait(pe, s_ttl, (T - 1).count())
                    project(T + 1, ps_b, slice(BANK, 2 * BANK), s_q[1])
                attend(Group(T - 1, 3))
                transpose_probs(Group(T, 1))
                scores(Group(T, 3))
                if (T + 1).live:
                    pe.wait_ge(s_kn, (T + 2).count())
                    pe.wait_ge(s_vl, (T + 2).count())
                    for g in range(KV_HEADS):
                        last = nc.tensor.transpose(ps_c[:, g * P:(g + 1) * P], k_nn[:, g].rearrange("p a d -> p (a d)"), ident[:])
                    last.then_inc(s_kt, 1)
                if (T - 1).live:
                    pe.wait_ge(s_yl, T.count(4))
                    out_project(T - 1, range(YC - 2, YC)).then_inc(s_o, 1)
                if (T + 1).live:
                    pe.wait_ge(s_ql[0], (T + 2).count())
                    transpose_q(T + 1, 0, ps_a)
                    pe.wait_ge(s_ql[1], (T + 2).count())
                    transpose_q(T + 1, 1, ps_b)
                attend(Group(T, 0))
                transpose_probs(Group(T, 2))
                scores(Group(T + 1, 0))
                if (T + 1).live:
                    pe.wait_ge(s_qT, (T + 1).count(4, 1))
                    transpose_q(T + 1, 2, ps_a)
                    pe.wait_ge(s_qT, (T + 1).count(4, 2))
                    transpose_q(T + 1, 3, ps_b)
                if (T - 1).live:
                    pe.wait_ge(s_hn, T.count())
                    wait(pe, s_ktl, min_count(T + 2))
                    for c in range(KC):
                        last = nc.tensor.transpose(ps_c[:, c * P:(c + 1) * P], hn[:, c * P:(c + 1) * P], ident[:])
                    last.then_inc(s_ht, 1)
                if (T + 2).live:
                    pe.wait_ge(s_xn, (T + 3).count())
                    wait(pe, s_ktl, (T + 2).count())
                    wait(pe, s_htl, T.count())
                    for c in range(KC):
                        last = nc.tensor.transpose(ps_c[:, c * P:(c + 1) * P], xn[:, c * P:(c + 1) * P], ident[:])
                    last.then_inc(s_xt, 1)
                if (T - 1).live:
                    pe.wait_ge(s_htl, T.count())
                    for c in range(KC):
                        last = three(ps_post[:, 0:FFN_OUT], hT_h[:, c], hT_l[:, c], wffn_h[:, c], wffn_l[:, c], c == 0, c == KC - 1)
                    last.then_inc(s_ffn, 1)
                attend(Group(T, 1))
                transpose_probs(Group(T, 3))
                scores(Group(T + 1, 1))
                if (T + 2).live:
                    pe.wait_ge(s_xtl, (T + 3).count())
                    project(T + 2, ps_c, slice(QDIM, QDIM + 2 * KVDIM), s_kv)
                if (T - 1).live:
                    pe.wait_ge(s_tg, T.count())
                    wait(pe, s_qT, min_count(T + 2, 4))
                    nc.tensor.transpose(ps_b[:, 0:P], tg[:].rearrange("p e r -> p (e r)"), ident[:]).then_inc(s_tt, 1)
                if (T + 2).live:
                    wait(pe, s_qT, (T + 1).count(4, 3))
                    project(T + 2, ps_a, slice(0, BANK), s_q[0])
                if (T - 1).live:
                    pe.wait_ge(s_ttl, T.count())
                    three(ps_post[:, 0:DIM], tgT_h[:], tgT_l[:], wv_h[:, 0], wv_l[:, 0], False, True, onto_ended=True).then_inc(s_lv, 1)
                attend(Group(T, 2))
                if T.k == -2:
                    pe.wait_ge(s_wl, len(WEIGHTS))

            steps(pe, step)

        


def min_count(tile, per=1):
    n = tile.count(per)
    return min(n, TILES * per) if isinstance(n, int) else n


def kernel(L0_attn_x, L0_attn_wq, L0_attn_wk, L0_attn_wv, L0_attn_wo, L0_attn_q_norm_w, L0_attn_k_norm_w,
           L0_ffn_weight, L0_ffn_gate_w, L0_ffn_lora_U, L0_ffn_lora_V):
    import numpy as np
    import concourse.bacc as bacc
    from concourse.bass_utils import run_bass_kernel_spmd

    as_np = np.asarray
    wo = as_np(L0_attn_wo).T.reshape(KV_HEADS, 2, 2, HD, DIM).transpose(0, 2, 1, 3, 4).reshape(QDIM, DIM)
    norm = np.stack([as_np(L0_attn_q_norm_w), as_np(L0_attn_k_norm_w)], axis=1)
    arrays = {
        "x": as_np(L0_attn_x).reshape(SEQS * SEQ_LEN, DIM),
        "w_qkv": np.concatenate([as_np(L0_attn_wq), as_np(L0_attn_wk), as_np(L0_attn_wv)], axis=0).T,
        "w_o": wo,
        "w_ffn": np.concatenate([as_np(L0_ffn_weight), as_np(L0_ffn_lora_U).reshape(ER, DIM), as_np(L0_ffn_gate_w)], axis=0).T,
        "w_v": as_np(L0_ffn_lora_V).transpose(0, 2, 1).reshape(ER, DIM),
        "norm_w": np.concatenate([norm, norm], axis=0),
    }
    arrays = {n: np.ascontiguousarray(a) for n, a in arrays.items()}
    nc = bacc.Bacc("TRN2", target_bir_lowering=False, num_devices=1)
    args = [nc.dram_tensor(n, a.shape, F32, kind="ExternalInput").ap() for n, a in arrays.items()]
    out = nc.dram_tensor("out", [SEQS * SEQ_LEN, DIM], F32, kind="ExternalOutput").ap()
    layer(nc, *args, out)
    r = run_bass_kernel_spmd(nc, [arrays], core_ids=[0])
    return r.results[0]["out"].reshape(SEQS, SEQ_LEN, DIM)
```

```python
import concourse.bass as bass
from concourse import mybir
from contextlib import ExitStack

F32 = mybir.dt.float32
F32R = mybir.dt.float32r
I32 = mybir.dt.int32
ALU = mybir.AluOpType
ACT = mybir.ActivationFunctionType
AX = mybir.AxisListType

P = 128
SEQS, SEQ_LEN, DIM = 32, 512, 256
HEADS, KV_HEADS, HD = 16, 4, 64
REP = HEADS // KV_HEADS
QDIM, KVDIM = HEADS * HD, KV_HEADS * HD
EXPERTS, RANK = 8, 16
ER = EXPERTS * RANK
FFN_OUT = DIM + ER + EXPERTS
KC = DIM // P
YC = QDIM // P
TPS = SEQ_LEN // P
TILES = SEQS * TPS
BANK = 512
LN_EPS, RMS_EPS = 1e-5, 1e-6
MASKED = -1e30
CONSTANTS = 7


class Tile:

    def __init__(self, j, k):
        self.j, self.k = j, k

    def __add__(self, d):
        return Tile(self.j, self.k + d)

    def __sub__(self, d):
        return Tile(self.j, self.k - d)

    @property
    def live(self):
        return not isinstance(self.j, int) or 0 <= TPS * self.j + self.k < TILES

    @property
    def slot(self):
        return self.k % TPS

    @property
    def par(self):
        return self.k % 2

    def count(self, per=1, more=0):
        return self.j * (TPS * per) + (self.k * per + more)

    def turn(self, ring):
        return self.j * (TPS // ring) + (self.k // ring + 1)


class Group:

    def __init__(self, tile, g):
        self.tile, self.g = tile + g // KV_HEADS, g % KV_HEADS

    @property
    def live(self):
        return self.tile.live

    @property
    def par(self):
        return self.g % 2

    def done(self, before=0):
        return self.tile.count(KV_HEADS, self.g + 1 - before)

    def prev_done(self):
        n, k = KV_HEADS * (TPS - 1), self.tile.k
        return self.tile.j * n + (k // TPS * n + (KV_HEADS * (k % TPS - 1) + self.g + 1 if k % TPS else 0))


def wait(eng, sem, value):
    if not isinstance(value, int) or value > 0:
        eng.wait_ge(sem, value)


def steps(eng, step):
    for T in range(-3, TPS):
        step(Tile(0, T))
    with eng.Fori(1, SEQS - 1) as j:
        for k in range(TPS):
            step(Tile(j, k))
    for T in range(TILES - TPS, TILES + 2):
        step(Tile(0, T))


def layer(nc, x, w_qkv, w_o, w_ffn, w_v, norm_w, out):
    ctx = ExitStack()
    with ctx:
        def sb(name, shape, dt=F32):
            return ctx.enter_context(nc.sbuf_tensor(name, shape, dt))

        def sem(name):
            return ctx.enter_context(nc.semaphore(name))

        wqkv_h, wqkv_l = (sb(f"wqkv_{n}", [P, KC, QDIM + 2 * KVDIM], F32R) for n in "hl")
        wo_h, wo_l = (sb(f"wo_{n}", [P, YC, DIM], F32R) for n in "hl")
        wffn_h, wffn_l = (sb(f"wffn_{n}", [P, KC, FFN_OUT], F32R) for n in "hl")
        wv_h, wv_l = (sb(f"wv_{n}", [P, 1, DIM], F32R) for n in "hl")
        w_plain = sb("w_plain", [P, KC * (QDIM + 2 * KVDIM)])
        nw = sb("nw", [P, 2])
        qk_w = sb("qk_w", [P, 1])
        ident, ident_r = sb("ident", [P, P]), sb("ident_r", [P, P], F32R)
        later_key = sb("later_key", [P, P])
        neg_later = sb("neg_later", [P, P])
        minus_half = sb("minus_half", [P, HEADS])
        pool_spare = sb("pool_spare", [P, KV_HEADS])
        xs = sb("xs", [P, TPS, DIM])
        x_stats, x_mv, x_ve, x_rstd = sb("x_stats", [P, 6]), sb("x_mv", [P, 2]), sb("x_ve", [P, 1]), sb("x_rstd", [P, 1])
        xn = sb("xn", [P, DIM])
        xT_h, xT_l = sb("xT_h", [P, KC, P], F32R), sb("xT_l", [P, KC, P], F32R)
        k_sq, k_ms, k_ve, k_r = sb("k_sq", [P, KVDIM]), sb("k_ms", [P, KV_HEADS]), sb("k_ve", [P, KV_HEADS]), sb("k_r", [P, KV_HEADS])
        q_sq = [sb(f"q_sq{n}", [P, BANK]) for n in range(2)]
        q_ms, q_ve, q_r = sb("q_ms", [P, HEADS]), sb("q_ve", [P, HEADS]), sb("q_r", [P, HEADS])
        k_nn = sb("k_nn", [P, KV_HEADS, 2, HD])
        q_n = sb("q_n", [P, HEADS, HD])
        q_hl = sb("q_hl", [P, HEADS, 2, HD], F32R)
        qT = sb("qT", [P, 2, HEADS, P], F32R)
        kT_h, kT_l = (sb(n, [P, KV_HEADS, (TPS + 1) * P], F32R) for n in ("kT_h", "kT_l"))
        vz_h, vz_l = (sb(n, [P, TPS, KV_HEADS, 3 * HD], F32R) for n in ("vz_h", "vz_l"))
        merged = sb("merged", [P, 2, REP, P])
        neg_max, den, rden = sb("neg_max", [P, 2, REP]), sb("den", [P, 2, REP]), sb("rden", [P, 2, REP])
        probs = sb("probs", [P, 2, REP, P])
        pT = sb("pT", [P, 2, 2, REP, P], F32R)
        pT_own, pT_prev = (sb(n, [P, 2, 2, REP, P], F32R) for n in ("pT_own", "pT_prev"))
        yT_h, yT_l = (sb(n, [P, 2, YC, P], F32R) for n in ("yT_h", "yT_l"))
        x1, hn = sb("x1", [P, DIM]), sb("hn", [P, DIM])
        h_stats, h_mv, h_ve, h_rstd = sb("h_stats", [P, 6]), sb("h_mv", [P, 2]), sb("h_ve", [P, 1]), sb("h_rstd", [P, 1])
        hT_h, hT_l = sb("hT_h", [P, KC, P], F32R), sb("hT_l", [P, KC, P], F32R)
        g_negmax, g_exp, g_den, g_rden, gate = sb("g_negmax", [P, 1]), sb("g_exp", [P, EXPERTS]), sb("g_den", [P, 1]), sb("g_rden", [P, 1]), sb("gate", [P, EXPERTS])
        tg = sb("tg", [P, EXPERTS, RANK])
        tgT_h, tgT_l = sb("tgT_h", [P, P], F32R), sb("tgT_l", [P, P], F32R)
        ob = sb("ob", [P, 2, DIM])

        ps_scores = ctx.enter_context(nc.psum_tensor("ps_scores", [P, REP, 2 * P], F32))
        ps_pT = ctx.enter_context(nc.psum_tensor("ps_pT", [P, REP, P], F32))
        ps_y = ctx.enter_context(nc.psum_tensor("ps_y", [P, BANK], F32))
        ps_post = ctx.enter_context(nc.psum_tensor("ps_post", [P, BANK], F32))
        ps_a, ps_b, ps_c = (ctx.enter_context(nc.psum_tensor(f"ps_{n}", [P, BANK], F32)) for n in "abc")

        s_w, s_nwl = sem("weights_loaded"), sem("norm_weights_loaded")
        s_wh, s_wl, s_const, s_ident_r, s_zero, s_nw = (sem(n) for n in ("weights_high", "weights_low", "constants_set", "ident_r_set", "zeros_set", "norm_product_set"))
        s_x = [sem(f"x_loaded{n}") for n in range(TPS)]
        s_xst, s_xmv, s_xve, s_xrstd, s_xn, s_xt, s_xth, s_xtl = (sem(n) for n in ("x_stats_done", "x_mean_done", "x_var_done", "x_rstd_done", "x_normed", "x_transposed", "xT_high", "xT_low"))
        s_kv, s_q = sem("kv_projected"), [sem(f"q{n}_projected") for n in range(2)]
        s_ksq, s_kms, s_kve, s_kr, s_kn = (sem(n) for n in ("k_squared", "k_summed", "k_mean_square", "k_rms_done", "k_normed"))
        s_vh, s_vl = sem("v_high"), sem("v_low")
        s_qsq, s_qms, s_qve, s_qr, s_qn, s_qh, s_ql = ([sem(f"q{n}_{what}") for n in range(2)] for what in ("squared", "summed", "mean_square", "rms_done", "normed", "high", "low"))
        s_kt, s_kth, s_ktl = sem("k_transposed"), sem("kT_high"), sem("kT_low")
        s_qt, s_qT = sem("q_transposed"), sem("qT_stored")
        s_s, s_own, s_merged, s_max, s_exp, s_rden, s_pn = (sem(n) for n in ("scores_done", "own_scores_copied", "scores_merged", "max_done", "exp_done", "rden_done", "probs_normed"))
        s_pt, s_ph, s_pl, s_po, s_pp, s_pv, s_yh, s_yl = (sem(n) for n in ("probs_transposed", "pT_high", "pT_low", "pT_own_done", "pT_prev_done", "pv_done", "yT_high", "yT_low"))
        s_o, s_x1, s_hst, s_hmv, s_hve, s_hrstd, s_hn, s_ht, s_hth, s_htl = (sem(n) for n in ("o_projected", "x1_done", "h_stats_done", "h_mean_done", "h_var_done", "h_rstd_done", "h_normed", "h_transposed", "hT_high", "hT_low"))
        s_ffn, s_gmax, s_gexp, s_grd, s_gate, s_tg, s_tt, s_tth, s_ttl, s_lv = (sem(n) for n in ("ffn_projected", "gate_max_done", "gate_exp_done", "gate_rden_done", "gate_done", "t_gated", "t_transposed", "tgT_high", "tgT_low", "lora_added"))
        s_ob = sem("out_ready")
        s_st = [sem(f"out_stored{n}") for n in range(2)]

        block = ctx.enter_context(nc.Block())
        WEIGHTS = [(w_qkv, wqkv_h, wqkv_l), (w_ffn, wffn_h, wffn_l), (w_o, wo_h, wo_l), (w_v, wv_h, wv_l)]

        def plain(h):
            _, c, n = h.shape
            return w_plain[:, 0:c * n].rearrange("p (c n) -> p c n", c=c)

        @block.sync
        def _(sp):
            def load_x(tile):
                sp.dma_start(xs[:, tile.slot, :], x[bass.ds(tile.count(P), P), :]).then_inc(s_x[tile.slot], 16)

            load_x(Tile(0, 0))
            sp.dma_start(nw[:], norm_w).then_inc(s_nwl, 16)
            for n, (w, h, _low) in enumerate(WEIGHTS):
                if n:
                    sp.wait_ge(s_wl, n)
                sp.dma_start(plain(h), w.rearrange("(c p) n -> p c n", p=P)).then_inc(s_w, 16)
            load_x(Tile(0, 1))
            load_x(Tile(0, 2))

            def step(T):
                if (T + 3).live and T.k >= 0:
                    wait(sp, s_x1, T.count())
                    load_x(T + 3)
                if (T - 2).live:
                    sp.wait_ge(s_ob, (T - 1).count())
                    sp.dma_start(out[bass.ds((T - 2).count(P), P), :], ob[:, (T - 2).par, :]).then_inc(s_st[(T - 2).par], 16)

            steps(sp, step)
            for n in range(2):
                sp.wait_ge(s_st[n], 16 * (TILES // 2))

        @block.gpsimd
        def _(pool):
            pool.memset(ident[:], 0.0).then_inc(s_const, 1)
            pool.memset(later_key[:], 0.0).then_inc(s_const, 1)
            pool.memset(neg_later[:], 0.0).then_inc(s_const, 1)
            pool.memset(minus_half[:], -0.5).then_inc(s_const, 1)
            pool.wait_ge(s_const, 4)
            pool.affine_select(out=ident[:], in_=ident[:], compare_op=ALU.not_equal, fill=1.0, base=0,
                               pattern=[[-1, P]], channel_multiplier=1).then_inc(s_const, 1)
            for m, fill in ((later_key, 1.0), (neg_later, MASKED)):
                pool.affine_select(out=m[:], in_=m[:], compare_op=ALU.is_ge, fill=fill, base=0,
                                   pattern=[[-1, P]], channel_multiplier=1).then_inc(s_const, 1)

            def split_probs(G):
                if not G.live:
                    return
                b = G.par
                src = pT[:, b].bitcast(F32).rearrange("p a h q -> p (a h) q")
                wait(pool, s_pl, G.done())
                wait(pool, s_pv, G.done(2))
                pool.tensor_tensor(pool_spare[:, G.g:G.g + 1], minus_half[:, 0:1], minus_half[:, 0:1], ALU.mult)
                pool.affine_select(out=pT_own[:, b].rearrange("p a h q -> p (a h) q"), in_=src, compare_op=ALU.is_ge,
                                   fill=0.0, base=0, pattern=[[0, 2 * REP], [1, P]], channel_multiplier=-1).then_inc(s_po, 1)
                if G.tile.slot:
                    pool.affine_select(out=pT_prev[:, b].rearrange("p a h q -> p (a h) q"), in_=src, compare_op=ALU.is_gt,
                                       fill=0.0, base=0, pattern=[[0, 2 * REP], [-1, P]], channel_multiplier=1).then_inc(s_pp, 1)

            def power(tile, ready, out_, in_, done):
                if tile.live:
                    pool.wait_ge(ready, (tile + 1).count())
                    n = in_.shape[-1]
                    pool.tensor_tensor(out_, in_, minus_half[:, 0:n], ALU.pow).then_inc(done, 1)

            def step(T):
                power(T + 1, s_qve[0], q_r[:, 0:8], q_ve[:, 0:8], s_qr[0])
                split_probs(Group(T, 0))
                power(T + 1, s_kve, k_r[:], k_ve[:], s_kr)
                split_probs(Group(T, 1))
                power(T + 1, s_qve[1], q_r[:, 8:16], q_ve[:, 8:16], s_qr[1])
                power(T - 1, s_hve, h_rstd[:], h_ve[:], s_hrstd)
                split_probs(Group(T, 2))
                split_probs(Group(T, 3))
                power(T + 3, s_xve, x_rstd[:], x_ve[:], s_xrstd)

            steps(pool, step)

        @block.scalar
        def _(act):
            for n, (_w, h, _low) in enumerate(WEIGHTS):
                act.wait_ge(s_w, 16 * (n + 1))
                nc.scalar.activation(h[:], plain(h), ACT.Copy).then_inc(s_wh, 1)

            def high_probs(G):
                if G.live:
                    act.wait_ge(s_pt, G.done())
                    wait(act, s_po, G.done(2))
                    wait(act, s_pp, Group(G.tile, G.g - 2).prev_done())
                    nc.scalar.activation(pT[:, G.par, 0], ps_pT[:], ACT.Copy).then_inc(s_ph, 1)

            def exps(G):
                if G.live:
                    act.wait_ge(s_max, G.done())
                    wait(act, s_pt, G.done(2))
                    for h in range(REP):
                        last = nc.scalar.activation(probs[:, G.par, h], merged[:, G.par, h], ACT.Exp,
                                                    bias=neg_max[:, G.par, h:h + 1], accum_out=den[:, G.par, h:h + 1])
                    last.then_inc(s_exp, 1)

            def own_scores(G):
                if G.live and G.tile.slot:
                    act.wait_ge(s_s, G.done())
                    wait(act, s_exp, G.done(2))
                    nc.scalar.activation(merged[:, G.par], ps_scores[:, :, P:2 * P], ACT.Copy).then_inc(s_own, 1)

            def high_y(G):
                if G.live:
                    act.wait_ge(s_pv, G.done())
                    nc.scalar.activation(yT_h[:, G.tile.par, 2 * G.g:2 * G.g + 2], ps_y[:, 0:2 * P].rearrange("p (c q) -> p c q", c=2), ACT.Copy).then_inc(s_yh, 1)

            def square_q(tile, n, ps):
                if tile.live:
                    act.wait_ge(s_q[n], (tile + 1).count())
                    nc.scalar.activation(q_sq[n][:], ps[:], ACT.Square).then_inc(s_qsq[n], 1)

            def store_qT(tile, n, ps):
                if tile.live:
                    act.wait_ge(s_qt, tile.count(4, n + 1))
                    nc.scalar.activation(qT[:, tile.par, 4 * n:4 * n + 4], ps[:].rearrange("p (h q) -> p h q", h=4), ACT.Copy).then_inc(s_qT, 1)

            def high_T(tile, ready, out_, ps, n, done):
                if tile.live:
                    act.wait_ge(ready, (tile + 1).count())
                    nc.scalar.activation(out_, ps[:, 0:n], ACT.Copy).then_inc(done, 1)

            def high_q(tile, n):
                if tile.live:
                    act.wait_ge(s_qn[n], (tile + 1).count())
                    wait(act, s_qt, tile.count(4, 2 * n + 2 - 4))
                    nc.scalar.activation(q_hl[:, 8 * n:8 * n + 8, 0], q_n[:, 8 * n:8 * n + 8], ACT.Copy).then_inc(s_qh[n], 1)

            def attention(probs_of, exps_of, y_of, own_of):
                high_probs(probs_of)
                exps(exps_of)
                high_y(y_of)
                own_scores(own_of)

            def step(T):
                attention(Group(T, 0), Group(T, 1), Group(T - 1, 3), Group(T, 2))
                high_T(T - 2, s_tt, tgT_h[:], ps_c, P, s_tth)
                if (T + 1).live:
                    act.wait_ge(s_kv, (T + 2).count())
                    nc.scalar.activation(k_sq[:], ps_a[:, 0:KVDIM], ACT.Square).then_inc(s_ksq, 1)
                    if T.k == -1:
                        act.wait_ge(s_zero, 1)
                    nc.scalar.activation(vz_h[:, (T + 1).slot, :, HD:2 * HD], ps_a[:, KVDIM:].rearrange("p (g d) -> p g d", g=KV_HEADS),
                                         ACT.Copy).then_inc(s_vh, 1)
                square_q(T + 1, 1, ps_c)
                high_q(T + 1, 0)
                attention(Group(T, 1), Group(T, 2), Group(T, 0), Group(T, 3))
                if (T + 1).live:
                    act.wait_ge(s_kt, (T + 2).count())
                    if T.k == -1:
                        act.wait_ge(s_nw, 1)
                    c = ((T + 1).slot + 1) * P
                    nc.scalar.activation(kT_h[:, :, c:c + P], ps_a[:].rearrange("p (g k) -> p g k", g=KV_HEADS), ACT.Copy,
                                         scale=qk_w[:, 0:1]).then_inc(s_kth, 1)
                store_qT(T + 1, 0, ps_b)
                attention(Group(T, 2), Group(T, 3), Group(T, 1), Group(T + 1, 0))
                high_T(T - 1, s_ht, hT_h[:].rearrange("p c q -> p (c q)"), ps_a, DIM, s_hth)
                store_qT(T + 1, 1, ps_b)
                high_q(T + 1, 1)
                high_T(T + 2, s_xt, xT_h[:].rearrange("p c q -> p (c q)"), ps_a, DIM, s_xth)
                attention(Group(T, 3), Group(T + 1, 0), Group(T, 2), Group(T + 1, 1))
                if (T - 1).live:
                    act.wait_ge(s_gmax, T.count())
                    nc.scalar.activation(g_exp[:], ps_post[:, DIM + ER:FFN_OUT], ACT.Exp, bias=g_negmax[:, 0:1],
                                         accum_out=g_den[:, 0:1]).then_inc(s_gexp, 1)
                store_qT(T + 1, 2, ps_c)
                store_qT(T + 1, 3, ps_a)
                square_q(T + 2, 0, ps_b)

            steps(act, step)

        @block.vector
        def _(dve):
            dve.wait_ge(s_const, CONSTANTS)
            nc.vector.tensor_copy(ident_r[:], ident[:]).then_inc(s_ident_r, 1)
            for m in (vz_h, vz_l):
                for s in range(TPS):
                    last = nc.vector.memset(m[:, s].bitcast(F32), 0.0)
            for m in (kT_h, kT_l):
                last = nc.vector.memset(m[:, :, 0:P].bitcast(F32), 0.0)
            last.then_inc(s_zero, 1)
            dve.wait_ge(s_nwl, 16)
            nc.vector.tensor_scalar(qk_w[:], nw[:, 0:1], nw[:, 1:2], float(HD) ** -0.5, ALU.mult, ALU.mult).then_inc(s_nw, 1)
            for n, (_w, h, low) in enumerate(WEIGHTS):
                dve.wait_ge(s_wh, n + 1)
                nc.vector.tensor_tensor(low[:], plain(h), h[:].bitcast(F32), ALU.subtract).then_inc(s_wl, 1)

            def mean_and_var(tile, st, mv, ve, s_st_, s_mv_, s_ve_):
                n = (tile + 1).count()
                if isinstance(n, int):
                    dve.wait_ge(s_st_, n)
                nc.vector.bn_aggr(mv[:], st[:]).then_inc(s_mv_, 1)
                dve.wait_ge(s_mv_, n)
                nc.vector.tensor_scalar_add(ve[:], mv[:, 1:2], LN_EPS).then_inc(s_ve_, 1)

            def low_probs(G):
                if G.live:
                    dve.wait_ge(s_ph, G.done())
                    nc.vector.tensor_tensor(pT[:, G.par, 1], ps_pT[:], pT[:, G.par, 0].bitcast(F32), ALU.subtract).then_inc(s_pl, 1)

            def merge(G):
                if not G.live:
                    return
                m = merged[:, G.par]
                every = [P, REP, P]
                if G.tile.slot:
                    n = G.prev_done()
                    if isinstance(n, int):
                        dve.wait_ge(s_own, n)
                    nc.vector.copy_predicated(m, later_key[:].bitcast(I32).unsqueeze(1).to_broadcast(every),
                                              ps_scores[:, :, 0:P]).then_inc(s_merged, 1)
                else:
                    dve.wait_ge(s_s, G.done())
                    wait(dve, s_exp, G.done(2))
                    nc.vector.tensor_tensor(m, ps_scores[:, :, P:2 * P], neg_later[:].unsqueeze(1).to_broadcast(every),
                                            ALU.add).then_inc(s_merged, 1)
                dve.wait_ge(s_merged, G.done())
                nc.vector.tensor_reduce(neg_max[:, G.par], m, AX.X, ALU.max, negate=True).then_inc(s_max, 1)

            def norm_probs(G):
                if G.live:
                    dve.wait_ge(s_exp, G.done())
                    nc.vector.reciprocal(rden[:, G.par], den[:, G.par]).then_inc(s_rden, 1)
                    dve.wait_ge(s_rden, G.done())
                    nc.vector.tensor_tensor(probs[:, G.par], probs[:, G.par], rden[:, G.par].unsqueeze(2).to_broadcast([P, REP, P]),
                                            ALU.mult).then_inc(s_pn, 1)

            def low_y(G, new):
                if G.live:
                    dve.wait_ge(s_yh, G.done())
                    if new.live and new.tile.slot:
                        dve.wait_ge(s_own, new.prev_done())
                    c = slice(2 * G.g, 2 * G.g + 2)
                    nc.vector.tensor_tensor(yT_l[:, G.tile.par, c], ps_y[:, 0:2 * P].rearrange("p (c q) -> p c q", c=2), yT_h[:, G.tile.par, c].bitcast(F32),
                                            ALU.subtract).then_inc(s_yl, 1)

            def mean_square(tile, sq, ms, ve, ready, s1, s2):
                if tile.live:
                    n = (tile + 1).count()
                    dve.wait_ge(ready, n)
                    nc.vector.reduce_sum(ms, sq.rearrange("p (h d) -> p h d", d=HD), AX.X).then_inc(s1, 1)
                    dve.wait_ge(s1, n)
                    nc.vector.tensor_scalar(ve, ms, 1.0 / HD, RMS_EPS, ALU.mult, ALU.add).then_inc(s2, 1)

            def norm_q(tile, n, ps):
                if tile.live:
                    c = slice(8 * n, 8 * n + 8)
                    dve.wait_ge(s_qr[n], (tile + 1).count())
                    nc.vector.tensor_tensor(q_n[:, c], ps[:].rearrange("p (h d) -> p h d", d=HD),
                                            q_r[:, c].unsqueeze(2).to_broadcast([P, 8, HD]), ALU.mult).then_inc(s_qn[n], 1)

            def low_q(tile, n):
                if tile.live:
                    c = slice(8 * n, 8 * n + 8)
                    dve.wait_ge(s_qh[n], (tile + 1).count())
                    nc.vector.tensor_tensor(q_hl[:, c, 1], q_n[:, c], q_hl[:, c, 0].bitcast(F32), ALU.subtract).then_inc(s_ql[n], 1)

            def low_T(tile, ready, out_, ps, n, hi, done):
                if tile.live:
                    dve.wait_ge(ready, (tile + 1).count())
                    nc.vector.tensor_tensor(out_, ps[:, 0:n], hi.bitcast(F32), ALU.subtract).then_inc(done, 1)

            def flat(a):
                return a[:].rearrange("p c q -> p (c q)")

            def attention(probs_of, exps_of, y_of, new):
                norm_probs(exps_of)
                low_y(y_of, new)
                merge(new)

            def step(T):
                mean_square(T + 1, q_sq[0][:], q_ms[:, 0:8], q_ve[:, 0:8], s_qsq[0], s_qms[0], s_qve[0])
                low_probs(Group(T, 0))
                low_T(T - 2, s_tth, tgT_l[:], ps_c, P, tgT_h[:], s_ttl)
                if (T + 2).live:
                    dve.wait_ge(s_xrstd, (T + 3).count())
                    nc.vector.tensor_scalar(xn[:], xs[:, (T + 2).slot], x_mv[:, 0:1], x_rstd[:, 0:1], ALU.subtract, ALU.mult).then_inc(s_xn, 1)
                attention(Group(T, 0), Group(T, 1), Group(T - 1, 3), Group(T, 2))
                mean_square(T + 1, k_sq[:], k_ms[:], k_ve[:], s_ksq, s_kms, s_kve)
                norm_q(T + 1, 0, ps_b)
                if (T + 1).live:
                    dve.wait_ge(s_vh, (T + 2).count())
                    s = (T + 1).slot
                    nc.vector.tensor_tensor(vz_l[:, s, :, HD:2 * HD], ps_a[:, KVDIM:].rearrange("p (g d) -> p g d", g=KV_HEADS),
                                            vz_h[:, s, :, HD:2 * HD].bitcast(F32), ALU.subtract).then_inc(s_vl, 1)
                if (T + 1).live:
                    dve.wait_ge(s_kr, (T + 2).count())
                    wait(dve, s_kt, (T + 1).count())
                    every = [P, KV_HEADS, 2, HD]
                    nc.vector.tensor_tensor(k_nn[:], ps_a[:, 0:KVDIM].rearrange("p (g d) -> p g d", g=KV_HEADS).unsqueeze(2).to_broadcast(every),
                                            k_r[:].unsqueeze(2).unsqueeze(3).to_broadcast(every), ALU.mult).then_inc(s_kn, 1)
                low_probs(Group(T, 1))
                low_q(T + 1, 0)
                if (T - 2).live:
                    dve.wait_ge(s_lv, (T - 1).count())
                    wait(dve, s_st[(T - 2).par], (T - 2).turn(2) * 16 - 16)
                    nc.vector.tensor_tensor(ob[:, (T - 2).par], ps_post[:, 0:DIM], x1[:], ALU.add).then_inc(s_ob, 1)
                attention(Group(T, 1), Group(T, 2), Group(T, 0), Group(T, 3))
                mean_square(T + 1, q_sq[1][:], q_ms[:, 8:16], q_ve[:, 8:16], s_qsq[1], s_qms[1], s_qve[1])
                if (T - 1).live:
                    dve.wait_ge(s_o, T.count())
                    nc.vector.tensor_tensor(x1[:], ps_post[:, 0:DIM], xs[:, (T - 1).slot], ALU.add).then_inc(s_x1, 1)
                    dve.wait_ge(s_x1, T.count())
                    nc.vector.bn_stats(h_stats[:], x1[:]).then_inc(s_hst, 1)
                    dve.wait_ge(s_hst, T.count())
                if (T + 1).live:
                    dve.wait_ge(s_kth, (T + 2).count())
                    c = ((T + 1).slot + 1) * P
                    nc.vector.scalar_tensor_tensor(kT_l[:, :, c:c + P], ps_a[:].rearrange("p (g k) -> p g k", g=KV_HEADS), qk_w[:, 0:1],
                                                   kT_h[:, :, c:c + P].bitcast(F32), op0=ALU.mult, op1=ALU.subtract).then_inc(s_ktl, 1)
                if (T - 1).live:
                    mean_and_var(T - 1, h_stats, h_mv, h_ve, s_hst, s_hmv, s_hve)
                norm_q(T + 1, 1, ps_c)
                low_probs(Group(T, 2))
                if (T - 1).live:
                    dve.wait_ge(s_hrstd, T.count())
                    nc.vector.tensor_scalar(hn[:], x1[:], h_mv[:, 0:1], h_rstd[:, 0:1], ALU.subtract, ALU.mult).then_inc(s_hn, 1)
                attention(Group(T, 2), Group(T, 3), Group(T, 1), Group(T + 1, 0))
                low_T(T - 1, s_hth, flat(hT_l), ps_a, DIM, flat(hT_h), s_htl)
                low_q(T + 1, 1)
                low_T(T + 2, s_xth, flat(xT_l), ps_a, DIM, flat(xT_h), s_xtl)
                low_probs(Group(T, 3))
                if (T - 1).live:
                    dve.wait_ge(s_ffn, T.count())
                    nc.vector.tensor_reduce(g_negmax[:], ps_post[:, DIM + ER:FFN_OUT], AX.X, ALU.max, negate=True).then_inc(s_gmax, 1)
                if (T + 3).live:
                    dve.wait_ge(s_x[(T + 3).slot], (T + 3).turn(TPS) * 16)
                    nc.vector.bn_stats(x_stats[:], xs[:, (T + 3).slot]).then_inc(s_xst, 1)
                attention(Group(T, 3), Group(T + 1, 0), Group(T, 2), Group(T + 1, 1))
                if (T + 3).live:
                    dve.wait_ge(s_xst, (T + 4).count())
                if (T - 1).live:
                    dve.wait_ge(s_gexp, T.count())
                    nc.vector.reciprocal(g_rden[:], g_den[:]).then_inc(s_grd, 1)
                    dve.wait_ge(s_grd, T.count())
                    nc.vector.tensor_scalar(gate[:], g_exp[:], g_rden[:, 0:1], 1.0 / RANK, ALU.mult, ALU.mult).then_inc(s_gate, 1)
                if (T + 3).live:
                    mean_and_var(T + 3, x_stats, x_mv, x_ve, s_xst, s_xmv, s_xve)
                if (T - 1).live:
                    dve.wait_ge(s_gate, T.count())
                    nc.vector.tensor_tensor(tg[:], ps_post[:, DIM:DIM + ER].rearrange("p (e r) -> p e r", e=EXPERTS),
                                            gate[:].unsqueeze(2).to_broadcast([P, EXPERTS, RANK]), ALU.mult).then_inc(s_tg, 1)

            steps(dve, step)

        @block.tensor
        def _(pe):
            def three(ps, stat_h, stat_l, mov_h, mov_l, first, last, onto_ended=False):
                nc.tensor.matmul(ps, stat_h, mov_h, start=first, stop=False, skip_group_check=onto_ended)
                nc.tensor.matmul(ps, stat_l, mov_h, start=False, stop=False, skip_group_check=onto_ended)
                return nc.tensor.matmul(ps, stat_h, mov_l, start=False, stop=last, skip_group_check=onto_ended)

            def transpose_probs(G):
                if G.live:
                    pe.wait_ge(s_pn, G.done())
                    wait(pe, s_pl, G.done(1))
                    for h in range(REP):
                        last = nc.tensor.transpose(ps_pT[:, h], probs[:, G.par, h], ident[:])
                    last.then_inc(s_pt, 1)

            def scores(G):
                if not G.live:
                    return
                T, g = G.tile, G.g
                pe.wait_ge(s_qT, T.count(4, g + 1))
                if g == 0:
                    pe.wait_ge(s_ktl, (T + 1).count())
                wait(pe, s_merged, G.done(1))
                keys = slice(T.slot * P, (T.slot + 2) * P)
                for h in range(REP):
                    q = qT[:, T.par, REP * g + h]
                    nc.tensor.matmul(ps_scores[:, h], q, kT_h[:, g, keys], start=True, stop=False)
                    last = nc.tensor.matmul(ps_scores[:, h], q, kT_l[:, g, keys], start=False, stop=True)
                last.then_inc(s_s, 1)

            def attend(G):
                if not G.live:
                    return
                T, g = G.tile, G.g
                wait(pe, s_yl, G.done(1))
                blocks = [(T.slot, pT_own)] + ([(T.slot - 1, pT_prev)] if T.slot else [])
                pe.wait_ge(s_po, G.done())
                if g == 0:
                    pe.wait_ge(s_vl, (T + 1).count())
                n = 0
                for s, pt in blocks:
                    if n:
                        pe.wait_ge(s_pp, G.prev_done())
                    for half in range(2):
                        cols = slice(HD - HD * half, HD - HD * half + P)
                        vh, vl = vz_h[:, s, g, cols], vz_l[:, s, g, cols]
                        ph, pl = (pt[:, G.par, m, 2 * half:2 * half + 2] for m in range(2))
                        for v, p in ((vh, ph), (vl, ph), (vh, pl)):
                            last = nc.tensor.matmul(ps_y[:, 0:2 * P], v, p, start=n == 0, stop=n == 6 * len(blocks) - 1)
                            n += 1
                last.then_inc(s_pv, 1)

            def project(ps, cols, done):
                for c in range(KC):
                    last = three(ps[:, 0:cols.stop - cols.start], xT_h[:, c], xT_l[:, c], wqkv_h[:, c, cols], wqkv_l[:, c, cols], c == 0, c == KC - 1)
                last.then_inc(done, 1)

            def transpose_q(n, ps):
                for h in range(4):
                    last = nc.tensor.transpose(ps[:, h * P:(h + 1) * P].bitcast(F32R), q_hl[:, 4 * n + h].rearrange("p a d -> p (a d)"), ident_r[:])
                last.then_inc(s_qt, 1)

            pe.wait_ge(s_const, CONSTANTS)
            pe.wait_ge(s_ident_r, 1)
            pe.wait_ge(s_zero, 1)
            pe.wait_ge(s_wl, 1)

            def attention(probs_of, y_of, new):
                transpose_probs(probs_of)
                attend(y_of)
                scores(new)

            def step(T):
                attention(Group(T, 0), Group(T - 1, 3), Group(T, 2))
                if (T - 2).live or (T + 1).live:
                    wait(pe, s_ttl, (T - 1).count())
                if (T + 1).live:
                    project(ps_c, slice(BANK, 2 * BANK), s_q[1])
                if (T - 2).live:
                    three(ps_post[:, 0:DIM], tgT_h[:], tgT_l[:], wv_h[:, 0], wv_l[:, 0], False, True, onto_ended=True).then_inc(s_lv, 1)
                attention(Group(T, 1), Group(T, 0), Group(T, 3))
                if (T + 1).live:
                    pe.wait_ge(s_kn, (T + 2).count())
                    pe.wait_ge(s_vl, (T + 2).count())
                    for g in range(KV_HEADS):
                        last = nc.tensor.transpose(ps_a[:, g * P:(g + 1) * P], k_nn[:, g].rearrange("p a d -> p (a d)"), ident[:])
                    last.then_inc(s_kt, 1)
                    pe.wait_ge(s_ql[0], (T + 2).count())
                    transpose_q(0, ps_b)
                if (T - 1).live:
                    pe.wait_ge(s_yl, T.count(4))
                    wait(pe, s_ob, (T - 1).count())
                    for c in range(YC):
                        last = three(ps_post[:, 0:DIM], yT_h[:, (T - 1).par, c], yT_l[:, (T - 1).par, c], wo_h[:, c], wo_l[:, c], c == 0, c == YC - 1)
                    last.then_inc(s_o, 1)
                attention(Group(T, 2), Group(T, 1), Group(T + 1, 0))
                if (T - 1).live:
                    pe.wait_ge(s_hn, T.count())
                    wait(pe, s_ktl, min_count(T + 2))
                    for c in range(KC):
                        last = nc.tensor.transpose(ps_a[:, c * P:(c + 1) * P], hn[:, c * P:(c + 1) * P], ident[:])
                    last.then_inc(s_ht, 1)
                if (T + 1).live:
                    pe.wait_ge(s_qT, (T + 1).count(4, 1))
                    transpose_q(1, ps_b)
                if (T + 2).live:
                    pe.wait_ge(s_xn, (T + 3).count())
                    wait(pe, s_ktl, (T + 2).count())
                    wait(pe, s_htl, T.count())
                    for c in range(KC):
                        last = nc.tensor.transpose(ps_a[:, c * P:(c + 1) * P], xn[:, c * P:(c + 1) * P], ident[:])
                    last.then_inc(s_xt, 1)
                if (T - 1).live:
                    pe.wait_ge(s_htl, T.count())
                    for c in range(KC):
                        last = three(ps_post[:, 0:FFN_OUT], hT_h[:, c], hT_l[:, c], wffn_h[:, c], wffn_l[:, c], c == 0, c == KC - 1)
                    last.then_inc(s_ffn, 1)
                attention(Group(T, 3), Group(T, 2), Group(T + 1, 1))
                if (T + 1).live:
                    pe.wait_ge(s_ql[1], (T + 2).count())
                    transpose_q(2, ps_c)
                    wait(pe, s_xtl, min_count(T + 3))
                    transpose_q(3, ps_a)
                if (T + 2).live:
                    wait(pe, s_xtl, (T + 3).count())
                    wait(pe, s_qT, (T + 1).count(4, 2))
                    project(ps_b, slice(0, BANK), s_q[0])
                    wait(pe, s_qT, (T + 1).count(4, 4))
                    project(ps_a, slice(QDIM, QDIM + 2 * KVDIM), s_kv)
                if (T - 1).live:
                    pe.wait_ge(s_tg, T.count())
                    wait(pe, s_qT, min_count(T + 2, 4))
                    nc.tensor.transpose(ps_c[:, 0:P], tg[:].rearrange("p e r -> p (e r)"), ident[:]).then_inc(s_tt, 1)
                if T.k == -2:
                    pe.wait_ge(s_wl, len(WEIGHTS))

            steps(pe, step)

        


def min_count(tile, per=1):
    n = tile.count(per)
    return min(n, TILES * per) if isinstance(n, int) else n


def kernel(L0_attn_x, L0_attn_wq, L0_attn_wk, L0_attn_wv, L0_attn_wo, L0_attn_q_norm_w, L0_attn_k_norm_w,
           L0_ffn_weight, L0_ffn_gate_w, L0_ffn_lora_U, L0_ffn_lora_V):
    import numpy as np
    import concourse.bacc as bacc
    from concourse.bass_utils import run_bass_kernel_spmd

    as_np = np.asarray
    wo = as_np(L0_attn_wo).T.reshape(KV_HEADS, 2, 2, HD, DIM).transpose(0, 2, 1, 3, 4).reshape(QDIM, DIM)
    norm = np.stack([as_np(L0_attn_q_norm_w), as_np(L0_attn_k_norm_w)], axis=1)
    arrays = {
        "x": as_np(L0_attn_x).reshape(SEQS * SEQ_LEN, DIM),
        "w_qkv": np.concatenate([as_np(L0_attn_wq), as_np(L0_attn_wk), as_np(L0_attn_wv)], axis=0).T,
        "w_o": wo,
        "w_ffn": np.concatenate([as_np(L0_ffn_weight), as_np(L0_ffn_lora_U).reshape(ER, DIM), as_np(L0_ffn_gate_w)], axis=0).T,
        "w_v": as_np(L0_ffn_lora_V).transpose(0, 2, 1).reshape(ER, DIM),
        "norm_w": np.concatenate([norm, norm], axis=0),
    }
    arrays = {n: np.ascontiguousarray(a) for n, a in arrays.items()}
    nc = bacc.Bacc("TRN2", target_bir_lowering=False, num_devices=1)
    args = [nc.dram_tensor(n, a.shape, F32, kind="ExternalInput").ap() for n, a in arrays.items()]
    out = nc.dram_tensor("out", [SEQS * SEQ_LEN, DIM], F32, kind="ExternalOutput").ap()
    layer(nc, *args, out)
    r = run_bass_kernel_spmd(nc, [arrays], core_ids=[0])
    return r.results[0]["out"].reshape(SEQS, SEQ_LEN, DIM)
```

```python
import concourse.bass as bass
from concourse import mybir
from contextlib import ExitStack

F32 = mybir.dt.float32
F32R = mybir.dt.float32r
I32 = mybir.dt.int32
ALU = mybir.AluOpType
ACT = mybir.ActivationFunctionType
AX = mybir.AxisListType

P = 128
SEQS, SEQ_LEN, DIM = 32, 512, 256
HEADS, KV_HEADS, HD = 16, 4, 64
REP = HEADS // KV_HEADS
QDIM, KVDIM = HEADS * HD, KV_HEADS * HD
EXPERTS, RANK = 8, 16
ER = EXPERTS * RANK
FFN_OUT = DIM + ER + EXPERTS
KC = DIM // P
YC = QDIM // P
TPS = SEQ_LEN // P
TILES = SEQS * TPS
BANK = 512
LN_EPS, RMS_EPS = 1e-5, 1e-6
MASKED = -1e30
O_EARLY = 4
NORM_BY_ACT = (2,)
CONSTANTS = 7


class Tile:

    def __init__(self, j, k):
        self.j, self.k = j, k

    def __add__(self, d):
        return Tile(self.j, self.k + d)

    def __sub__(self, d):
        return Tile(self.j, self.k - d)

    @property
    def live(self):
        return not isinstance(self.j, int) or 0 <= TPS * self.j + self.k < TILES

    @property
    def slot(self):
        return self.k % TPS

    @property
    def par(self):
        return self.k % 2

    def count(self, per=1, more=0):
        return self.j * (TPS * per) + (self.k * per + more)

    def turn(self, ring):
        return self.j * (TPS // ring) + (self.k // ring + 1)


class Group:

    def __init__(self, tile, g):
        self.tile, self.g = tile + g // KV_HEADS, g % KV_HEADS

    @property
    def live(self):
        return self.tile.live

    @property
    def par(self):
        return self.g % 2

    def done(self, before=0):
        return self.tile.count(KV_HEADS, self.g + 1 - before)

    def prev_done(self):
        n, k = KV_HEADS * (TPS - 1), self.tile.k
        return self.tile.j * n + (k // TPS * n + (KV_HEADS * (k % TPS - 1) + self.g + 1 if k % TPS else 0))


def wait(eng, sem, value):
    if not isinstance(value, int) or value > 0:
        eng.wait_ge(sem, value)


def steps(eng, step):
    for T in range(-3, TPS):
        step(Tile(0, T))
    with eng.Fori(1, SEQS - 1) as j:
        for k in range(TPS):
            step(Tile(j, k))
    for T in range(TILES - TPS, TILES + 2):
        step(Tile(0, T))


def layer(nc, x, w_qkv, w_o, w_ffn, w_v, norm_w, out):
    ctx = ExitStack()
    with ctx:
        def sb(name, shape, dt=F32):
            return ctx.enter_context(nc.sbuf_tensor(name, shape, dt))

        def sem(name):
            return ctx.enter_context(nc.semaphore(name))

        wqkv_h, wqkv_l = (sb(f"wqkv_{n}", [P, KC, QDIM + 2 * KVDIM], F32R) for n in "hl")
        wo_h, wo_l = (sb(f"wo_{n}", [P, YC, DIM], F32R) for n in "hl")
        wffn_h, wffn_l = (sb(f"wffn_{n}", [P, KC, FFN_OUT], F32R) for n in "hl")
        wv_h, wv_l = (sb(f"wv_{n}", [P, 1, DIM], F32R) for n in "hl")
        w_plain = sb("w_plain", [P, KC * FFN_OUT + YC * DIM + DIM])
        nw = sb("nw", [P, 2])
        qk_w = sb("qk_w", [P, 1])
        ident, ident_r = sb("ident", [P, P]), sb("ident_r", [P, P], F32R)
        later_key = sb("later_key", [P, P])
        neg_later = sb("neg_later", [P, P])
        minus_half = sb("minus_half", [P, HEADS])
        pool_spare = sb("pool_spare", [P, KV_HEADS])
        xs = sb("xs", [P, TPS, DIM])
        x_stats, x_mv, x_ve, x_rstd = sb("x_stats", [P, 6]), sb("x_mv", [P, 2]), sb("x_ve", [P, 1]), sb("x_rstd", [P, 1])
        xc, xn = sb("xc", [P, DIM]), sb("xn", [P, DIM])
        xT_h, xT_l = sb("xT_h", [P, KC, P], F32R), sb("xT_l", [P, KC, P], F32R)
        k_sq, k_ms, k_ve, k_r = sb("k_sq", [P, KVDIM]), sb("k_ms", [P, KV_HEADS]), sb("k_ve", [P, KV_HEADS]), sb("k_r", [P, KV_HEADS])
        q_sq = [sb(f"q_sq{n}", [P, BANK]) for n in range(2)]
        q_ms, q_ve, q_r = sb("q_ms", [P, HEADS]), sb("q_ve", [P, HEADS]), sb("q_r", [P, HEADS])
        k_nn = sb("k_nn", [P, KV_HEADS, 2, HD])
        q_n = sb("q_n", [P, HEADS, HD])
        q_hl = sb("q_hl", [P, HEADS, 2, HD], F32R)
        qT = sb("qT", [P, 2, HEADS, P], F32R)
        kT_h, kT_l = (sb(n, [P, KV_HEADS, (TPS + 1) * P], F32R) for n in ("kT_h", "kT_l"))
        vz_h, vz_l = (sb(n, [P, TPS, KV_HEADS, 3 * HD], F32R) for n in ("vz_h", "vz_l"))
        merged = sb("merged", [P, 2, REP, P])
        neg_max, den, rden = sb("neg_max", [P, 2, REP]), sb("den", [P, 2, REP]), sb("rden", [P, 2, REP])
        probs = sb("probs", [P, 2, REP, P])
        pT = sb("pT", [P, 2, 2, REP, P], F32R)
        pT_own, pT_prev = (sb(n, [P, 2, 2, REP, P], F32R) for n in ("pT_own", "pT_prev"))
        yT_h, yT_l = (sb(n, [P, 2, YC, P], F32R) for n in ("yT_h", "yT_l"))
        x1, hn = sb("x1", [P, DIM]), sb("hn", [P, DIM])
        h_stats, h_mv, h_ve, h_rstd = sb("h_stats", [P, 6]), sb("h_mv", [P, 2]), sb("h_ve", [P, 1]), sb("h_rstd", [P, 1])
        hT_h, hT_l = sb("hT_h", [P, KC, P], F32R), sb("hT_l", [P, KC, P], F32R)
        g_negmax, g_exp, g_den, g_rden, gate = sb("g_negmax", [P, 1]), sb("g_exp", [P, EXPERTS]), sb("g_den", [P, 1]), sb("g_rden", [P, 1]), sb("gate", [P, EXPERTS])
        tg = sb("tg", [P, EXPERTS, RANK])
        tgT_h, tgT_l = sb("tgT_h", [P, P], F32R), sb("tgT_l", [P, P], F32R)
        ob = sb("ob", [P, 2, DIM])

        ps_scores = ctx.enter_context(nc.psum_tensor("ps_scores", [P, REP, 2 * P], F32))
        ps_pT = ctx.enter_context(nc.psum_tensor("ps_pT", [P, REP, P], F32))
        ps_y = ctx.enter_context(nc.psum_tensor("ps_y", [P, BANK], F32))
        ps_post = ctx.enter_context(nc.psum_tensor("ps_post", [P, BANK], F32))
        ps_a, ps_b, ps_c = (ctx.enter_context(nc.psum_tensor(f"ps_{n}", [P, BANK], F32)) for n in "abc")

        s_w, s_nwl = [sem(f"weight{n}_loaded") for n in range(6)], sem("norm_weights_loaded")
        s_wh, s_wl, s_const, s_ident_r, s_zero, s_nw = (sem(n) for n in ("weights_high", "weights_low", "constants_set", "ident_r_set", "zeros_set", "norm_product_set"))
        s_x = [sem(f"x_loaded{n}") for n in range(TPS)]
        s_xst, s_xmv, s_xve, s_xrstd, s_xc, s_xn, s_xt, s_xth, s_xtl = (sem(n) for n in ("x_stats_done", "x_mean_done", "x_var_done", "x_rstd_done", "x_centred", "x_normed", "x_transposed", "xT_high", "xT_low"))
        s_kv, s_q = sem("kv_projected"), [sem(f"q{n}_projected") for n in range(2)]
        s_ksq, s_kms, s_kve, s_kr, s_kn = (sem(n) for n in ("k_squared", "k_summed", "k_mean_square", "k_rms_done", "k_normed"))
        s_vh, s_vl = sem("v_high"), sem("v_low")
        s_qsq, s_qms, s_qve, s_qr, s_qn, s_qh, s_ql = ([sem(f"q{n}_{what}") for n in range(2)] for what in ("squared", "summed", "mean_square", "rms_done", "normed", "high", "low"))
        s_kt, s_kth, s_ktl = sem("k_transposed"), sem("kT_high"), sem("kT_low")
        s_qt, s_qT = sem("q_transposed"), sem("qT_stored")
        s_s, s_own, s_merged, s_max, s_exp, s_rden, s_pn = (sem(n) for n in ("scores_done", "own_scores_copied", "scores_merged", "max_done", "exp_done", "rden_done", "probs_normed"))
        s_pt, s_ph, s_pl, s_po, s_pp, s_pv, s_yh, s_yl = (sem(n) for n in ("probs_transposed", "pT_high", "pT_low", "pT_own_done", "pT_prev_done", "pv_done", "yT_high", "yT_low"))
        s_o, s_x1, s_hst, s_hmv, s_hve, s_hrstd, s_hn, s_ht, s_hth, s_htl = (sem(n) for n in ("o_projected", "x1_done", "h_stats_done", "h_mean_done", "h_var_done", "h_rstd_done", "h_normed", "h_transposed", "hT_high", "hT_low"))
        s_ffn, s_gmax, s_gexp, s_grd, s_gate, s_tg, s_tt, s_tth, s_ttl, s_lv = (sem(n) for n in ("ffn_projected", "gate_max_done", "gate_exp_done", "gate_rden_done", "gate_done", "t_gated", "t_transposed", "tgT_high", "tgT_low", "lora_added"))
        s_ob = sem("out_ready")
        s_st = [sem(f"out_stored{n}") for n in range(2)]

        block = ctx.enter_context(nc.Block())
        WEIGHTS = []
        for n, c in enumerate((slice(0, BANK), slice(QDIM, QDIM + 2 * KVDIM), slice(BANK, 2 * BANK))):
            WEIGHTS.append((w_qkv[:, c], wqkv_h[:, :, c], wqkv_l[:, :, c], n * KC * BANK))
        WEIGHTS += [(w_ffn, wffn_h[:], wffn_l[:], 0), (w_o, wo_h[:], wo_l[:], KC * FFN_OUT), (w_v, wv_h[:], wv_l[:], KC * FFN_OUT + YC * DIM)]
        QKV = 3

        def plain(n):
            _w, high, _low, at = WEIGHTS[n]
            _, c, cols = high.shape
            return w_plain[:, at:at + c * cols].rearrange("p (c n) -> p c n", c=c)

        @block.sync
        def _(sp):
            def load_x(tile):
                sp.dma_start(xs[:, tile.slot, :], x[bass.ds(tile.count(P), P), :]).then_inc(s_x[tile.slot], 16)

            def load_weight(n):
                sp.dma_start(plain(n), WEIGHTS[n][0].rearrange("(c p) n -> p c n", p=P)).then_inc(s_w[n], 16)

            load_x(Tile(0, 0))
            load_weight(0)
            load_weight(1)
            load_weight(2)
            sp.dma_start(nw[:], norm_w).then_inc(s_nwl, 16)
            load_x(Tile(0, 1))
            load_x(Tile(0, 2))
            sp.wait_ge(s_wl, QKV)
            for n in range(QKV, len(WEIGHTS)):
                load_weight(n)

            def step(T):
                if (T + 3).live and T.k >= 0:
                    wait(sp, s_x1, T.count())
                    load_x(T + 3)
                if (T - 2).live:
                    sp.wait_ge(s_ob, (T - 1).count())
                    sp.dma_start(out[bass.ds((T - 2).count(P), P), :], ob[:, (T - 2).par, :]).then_inc(s_st[(T - 2).par], 16)

            steps(sp, step)
            for n in range(2):
                sp.wait_ge(s_st[n], 16 * (TILES // 2))

        @block.gpsimd
        def _(pool):
            pool.memset(ident[:], 0.0).then_inc(s_const, 1)
            pool.memset(later_key[:], 0.0).then_inc(s_const, 1)
            pool.memset(neg_later[:], 0.0).then_inc(s_const, 1)
            pool.memset(minus_half[:], -0.5).then_inc(s_const, 1)
            pool.wait_ge(s_const, 4)
            pool.affine_select(out=ident[:], in_=ident[:], compare_op=ALU.not_equal, fill=1.0, base=0,
                               pattern=[[-1, P]], channel_multiplier=1).then_inc(s_const, 1)
            for m, fill in ((later_key, 1.0), (neg_later, MASKED)):
                pool.affine_select(out=m[:], in_=m[:], compare_op=ALU.is_ge, fill=fill, base=0,
                                   pattern=[[-1, P]], channel_multiplier=1).then_inc(s_const, 1)

            def set_zeros():
                for m in (kT_h, kT_l):
                    pool.memset(m[:, :, 0:P].bitcast(F32), 0.0)
                for m in (vz_h, vz_l):
                    for c in (0, 2 * HD):
                        last = pool.memset(m[:, :, :, c:c + HD].rearrange("p s g d -> p (s g) d").bitcast(F32), 0.0)
                last.then_inc(s_zero, 1)

            def split_probs(G):
                if not G.live:
                    return
                b = G.par
                src = pT[:, b].bitcast(F32).rearrange("p a h q -> p (a h) q")
                wait(pool, s_pl, G.done())
                wait(pool, s_pv, G.done(2))
                pool.tensor_tensor(pool_spare[:, G.g:G.g + 1], minus_half[:, 0:1], minus_half[:, 0:1], ALU.mult)
                pool.affine_select(out=pT_own[:, b].rearrange("p a h q -> p (a h) q"), in_=src, compare_op=ALU.is_ge,
                                   fill=0.0, base=0, pattern=[[0, 2 * REP], [1, P]], channel_multiplier=-1).then_inc(s_po, 1)
                if G.tile.slot:
                    pool.affine_select(out=pT_prev[:, b].rearrange("p a h q -> p (a h) q"), in_=src, compare_op=ALU.is_gt,
                                       fill=0.0, base=0, pattern=[[0, 2 * REP], [-1, P]], channel_multiplier=1).then_inc(s_pp, 1)

            def power(tile, ready, out_, in_, done):
                if tile.live:
                    pool.wait_ge(ready, (tile + 1).count())
                    n = in_.shape[-1]
                    pool.tensor_tensor(out_, in_, minus_half[:, 0:n], ALU.pow).then_inc(done, 1)

            def low_q(tile, n):
                if tile.live:
                    c = slice(8 * n, 8 * n + 8)
                    pool.wait_ge(s_qh[n], (tile + 1).count())
                    pool.tensor_tensor(q_hl[:, c, 1], q_n[:, c], q_hl[:, c, 0].bitcast(F32), ALU.subtract).then_inc(s_ql[n], 1)

            def step(T):
                split_probs(Group(T, 0))
                if T.k == -2:
                    set_zeros()
                power(T + 1, s_kve, k_r[:], k_ve[:], s_kr)
                low_q(T + 1, 0)
                split_probs(Group(T, 1))
                power(T + 1, s_qve[1], q_r[:, 8:16], q_ve[:, 8:16], s_qr[1])
                power(T - 1, s_hve, h_rstd[:], h_ve[:], s_hrstd)
                split_probs(Group(T, 2))
                low_q(T + 1, 1)
                split_probs(Group(T, 3))
                power(T + 3, s_xve, x_rstd[:], x_ve[:], s_xrstd)
                if (T + 3).live:
                    wait(pool, s_xt, (T + 3).count())
                    pool.tensor_tensor(xc[:], xs[:, (T + 3).slot], x_mv[:, 0:1].to_broadcast([P, DIM]), ALU.subtract).then_inc(s_xc, 1)
                power(T + 2, s_qve[0], q_r[:, 0:8], q_ve[:, 0:8], s_qr[0])
                if (T + 3).live:
                    pool.wait_ge(s_xrstd, (T + 4).count())
                    pool.wait_ge(s_xc, (T + 4).count())
                    pool.tensor_tensor(xn[:], xc[:], x_rstd[:, 0:1].to_broadcast([P, DIM]), ALU.mult).then_inc(s_xn, 1)

            steps(pool, step)

        @block.scalar
        def _(act):
            def high_weights(first, end):
                for n in range(first, end):
                    act.wait_ge(s_w[n], 16)
                    nc.scalar.activation(WEIGHTS[n][1], plain(n), ACT.Copy).then_inc(s_wh, 1)

            high_weights(0, 1)

            def high_probs(G):
                if G.live:
                    act.wait_ge(s_pt, G.done())
                    wait(act, s_po, G.done(2))
                    wait(act, s_pp, Group(G.tile, G.g - 2).prev_done())
                    nc.scalar.activation(pT[:, G.par, 0], ps_pT[:], ACT.Copy).then_inc(s_ph, 1)

            def exps(G, half):
                if G.live:
                    if not half:
                        act.wait_ge(s_max, G.done())
                        wait(act, s_pt, G.done(2))
                    for h in range(2 * half, 2 * half + 2):
                        last = nc.scalar.activation(probs[:, G.par, h], merged[:, G.par, h], ACT.Exp,
                                                    bias=neg_max[:, G.par, h:h + 1], accum_out=den[:, G.par, h:h + 1])
                    last.then_inc(s_exp, 1)

            def normalise(G):
                if G.live and G.g in NORM_BY_ACT:
                    act.wait_ge(s_rden, G.done())
                    for h in range(REP):
                        last = nc.scalar.activation(probs[:, G.par, h], probs[:, G.par, h], ACT.Copy, scale=rden[:, G.par, h:h + 1])
                    last.then_inc(s_pn, 1)

            def own_scores(G):
                if G.live and G.tile.slot:
                    act.wait_ge(s_s, G.done())
                    wait(act, s_exp, 2 * G.done(2))
                    nc.scalar.activation(merged[:, G.par], ps_scores[:, :, P:2 * P], ACT.Copy).then_inc(s_own, 1)

            def high_y(G):
                if G.live:
                    act.wait_ge(s_pv, G.done())
                    nc.scalar.activation(yT_h[:, G.tile.par, 2 * G.g:2 * G.g + 2], ps_y[:, 0:2 * P].rearrange("p (c q) -> p c q", c=2), ACT.Copy).then_inc(s_yh, 1)

            def square_q(tile, n, ps):
                if tile.live:
                    act.wait_ge(s_q[n], (tile + 1).count())
                    nc.scalar.activation(q_sq[n][:], ps[:], ACT.Square).then_inc(s_qsq[n], 1)

            def store_qT(tile, n, ps):
                if tile.live:
                    act.wait_ge(s_qt, tile.count(4, n + 1))
                    nc.scalar.activation(qT[:, tile.par, 4 * n:4 * n + 4], ps[:].rearrange("p (h q) -> p h q", h=4), ACT.Copy).then_inc(s_qT, 1)

            def high_T(tile, ready, out_, ps, done):
                if tile.live:
                    act.wait_ge(ready, (tile + 1).count())
                    nc.scalar.activation(out_, ps[:, 0:out_.shape[-1]], ACT.Copy).then_inc(done, 1)

            def high_q(tile, n):
                if tile.live:
                    act.wait_ge(s_qn[n], (tile + 1).count())
                    wait(act, s_qt, tile.count(4, 2 * n + 2 - 4))
                    nc.scalar.activation(q_hl[:, 8 * n:8 * n + 8, 0], q_n[:, 8 * n:8 * n + 8], ACT.Copy).then_inc(s_qh[n], 1)

            def step(T):
                if T.k == -2:
                    high_weights(1, QKV)
                high_probs(Group(T, 0))
                exps(Group(T, 1), 0)
                if T.k == -1:
                    high_weights(QKV, len(WEIGHTS))
                exps(Group(T, 1), 1)
                high_T(T - 2, s_tt, tgT_h[:], ps_y[:, 2 * P:3 * P], s_tth)
                if (T + 1).live:
                    act.wait_ge(s_kv, (T + 2).count())
                    nc.scalar.activation(k_sq[:], ps_b[:, 0:KVDIM], ACT.Square).then_inc(s_ksq, 1)
                high_y(Group(T - 1, 3))
                if (T + 1).live:
                    if T.k == -1:
                        act.wait_ge(s_zero, 1)
                    nc.scalar.activation(vz_h[:, (T + 1).slot, :, HD:2 * HD], ps_b[:, KVDIM:].rearrange("p (g d) -> p g d", g=KV_HEADS),
                                         ACT.Copy).then_inc(s_vh, 1)
                own_scores(Group(T, 2))
                normalise(Group(T, 1))
                square_q(T + 1, 1, ps_c)
                high_q(T + 1, 0)
                high_probs(Group(T, 1))
                exps(Group(T, 2), 0)
                exps(Group(T, 2), 1)
                high_y(Group(T, 0))
                high_T(T + 2, s_xt, xT_h[:].rearrange("p c q -> p (c q)"), ps_y[:, 2 * P:4 * P], s_xth)
                own_scores(Group(T, 3))
                normalise(Group(T, 2))
                if (T + 1).live:
                    act.wait_ge(s_kt, (T + 2).count())
                    if T.k == -1:
                        act.wait_ge(s_nw, 1)
                    c = ((T + 1).slot + 1) * P
                    nc.scalar.activation(kT_h[:, :, c:c + P], ps_a[:].rearrange("p (g k) -> p g k", g=KV_HEADS), ACT.Copy,
                                         scale=qk_w[:, 0:1]).then_inc(s_kth, 1)
                store_qT(T + 1, 0, ps_b)
                high_probs(Group(T, 2))
                exps(Group(T, 3), 0)
                exps(Group(T, 3), 1)
                own_scores(Group(T + 1, 0))
                high_y(Group(T, 1))
                store_qT(T + 1, 1, ps_b)
                high_q(T + 1, 1)
                normalise(Group(T, 3))
                normalise(Group(T + 1, 0))
                high_T(T - 1, s_ht, hT_h[:].rearrange("p c q -> p (c q)"), ps_b, s_hth)
                square_q(T + 2, 0, ps_a)
                exps(Group(T + 1, 0), 0)
                high_probs(Group(T, 3))
                high_y(Group(T, 2))
                exps(Group(T + 1, 0), 1)
                own_scores(Group(T + 1, 1))
                store_qT(T + 1, 2, ps_b)
                store_qT(T + 1, 3, ps_c)
                if (T - 1).live:
                    act.wait_ge(s_gmax, T.count())
                    nc.scalar.activation(g_exp[:], ps_post[:, DIM + ER:FFN_OUT], ACT.Exp, bias=g_negmax[:, 0:1],
                                         accum_out=g_den[:, 0:1]).then_inc(s_gexp, 1)

            steps(act, step)

        @block.vector
        def _(dve):
            dve.wait_ge(s_const, CONSTANTS)
            nc.vector.tensor_copy(ident_r[:], ident[:]).then_inc(s_ident_r, 1)
            def low_weights(first, end):
                for n in range(first, end):
                    dve.wait_ge(s_wh, n + 1)
                    nc.vector.tensor_tensor(WEIGHTS[n][2], plain(n), WEIGHTS[n][1].bitcast(F32), ALU.subtract).then_inc(s_wl, 1)

            def mean_and_var(tile, st, mv, ve, s_st_, s_mv_, s_ve_):
                if tile.live:
                    n = (tile + 1).count()
                    if isinstance(n, int):
                        dve.wait_ge(s_st_, n)
                    nc.vector.bn_aggr(mv[:], st[:]).then_inc(s_mv_, 1)
                    dve.wait_ge(s_mv_, n)
                    nc.vector.tensor_scalar_add(ve[:], mv[:, 1:2], LN_EPS).then_inc(s_ve_, 1)

            def low_probs(G):
                if G.live:
                    dve.wait_ge(s_ph, G.done())
                    nc.vector.tensor_tensor(pT[:, G.par, 1], ps_pT[:], pT[:, G.par, 0].bitcast(F32), ALU.subtract).then_inc(s_pl, 1)

            def wait_own(G):
                if G.live and G.tile.slot:
                    dve.wait_ge(s_own, G.prev_done())

            def merge(G):
                if G.live:
                    m = merged[:, G.par]
                    every = [P, REP, P]
                    if G.tile.slot:
                        nc.vector.copy_predicated(m, later_key[:].bitcast(I32).unsqueeze(1).to_broadcast(every),
                                                  ps_scores[:, :, 0:P]).then_inc(s_merged, 1)
                    else:
                        dve.wait_ge(s_s, G.done())
                        wait(dve, s_exp, 2 * G.done(2))
                        nc.vector.tensor_tensor(m, ps_scores[:, :, P:2 * P], neg_later[:].unsqueeze(1).to_broadcast(every),
                                                ALU.add).then_inc(s_merged, 1)

            def maximum(G):
                if G.live:
                    dve.wait_ge(s_merged, G.done())
                    nc.vector.tensor_reduce(neg_max[:, G.par], merged[:, G.par], AX.X, ALU.max, negate=True).then_inc(s_max, 1)

            def inverse(G):
                if G.live:
                    dve.wait_ge(s_exp, G.done() * 2)
                    nc.vector.reciprocal(rden[:, G.par], den[:, G.par]).then_inc(s_rden, 1)

            def norm_probs(G):
                if G.live and G.g not in NORM_BY_ACT:
                    dve.wait_ge(s_rden, G.done())
                    nc.vector.tensor_tensor(probs[:, G.par], probs[:, G.par], rden[:, G.par].unsqueeze(2).to_broadcast([P, REP, P]),
                                            ALU.mult).then_inc(s_pn, 1)

            def low_y(G):
                if G.live:
                    dve.wait_ge(s_yh, G.done())
                    c = slice(2 * G.g, 2 * G.g + 2)
                    nc.vector.tensor_tensor(yT_l[:, G.tile.par, c], ps_y[:, 0:2 * P].rearrange("p (c q) -> p c q", c=2), yT_h[:, G.tile.par, c].bitcast(F32),
                                            ALU.subtract).then_inc(s_yl, 1)

            def sum_squares(tile, sq, ms, ready, done):
                if tile.live:
                    dve.wait_ge(ready, (tile + 1).count())
                    nc.vector.reduce_sum(ms, sq.rearrange("p (h d) -> p h d", d=HD), AX.X).then_inc(done, 1)

            def mean_square(tile, ms, ve, ready, done):
                if tile.live:
                    dve.wait_ge(ready, (tile + 1).count())
                    nc.vector.tensor_scalar(ve, ms, 1.0 / HD, RMS_EPS, ALU.mult, ALU.add).then_inc(done, 1)

            def norm_q(tile, n, ps):
                if tile.live:
                    c = slice(8 * n, 8 * n + 8)
                    dve.wait_ge(s_qr[n], (tile + 1).count())
                    nc.vector.tensor_tensor(q_n[:, c], ps[:].rearrange("p (h d) -> p h d", d=HD),
                                            q_r[:, c].unsqueeze(2).to_broadcast([P, 8, HD]), ALU.mult).then_inc(s_qn[n], 1)

            def low_T(tile, ready, out_, ps, hi, done):
                if tile.live:
                    n = out_.shape[-1]
                    dve.wait_ge(ready, (tile + 1).count())
                    nc.vector.tensor_tensor(out_, ps[:, 0:n], hi.bitcast(F32), ALU.subtract).then_inc(done, 1)

            def flat(a):
                return a[:].rearrange("p c q -> p (c q)")

            def step(T):
                if T.k == -2:
                    low_weights(0, QKV)
                low_probs(Group(T, 0))
                inverse(Group(T, 1))
                norm_probs(Group(T, 1))
                low_y(Group(T - 1, 3))
                if T.k == -1:
                    low_weights(QKV, len(WEIGHTS))
                    dve.wait_ge(s_nwl, 16)
                    nc.vector.tensor_scalar(qk_w[:], nw[:, 0:1], nw[:, 1:2], float(HD) ** -0.5, ALU.mult, ALU.mult).then_inc(s_nw, 1)
                low_T(T - 2, s_tth, tgT_l[:], ps_y[:, 2 * P:3 * P], tgT_h[:], s_ttl)
                norm_q(T + 1, 0, ps_a)
                if (T - 2).live:
                    dve.wait_ge(s_lv, (T - 1).count())
                    wait(dve, s_st[(T - 2).par], (T - 2).turn(2) * 16 - 16)
                    nc.vector.tensor_tensor(ob[:, (T - 2).par], ps_post[:, 0:DIM], x1[:], ALU.add).then_inc(s_ob, 1)
                wait_own(Group(T, 2))
                sum_squares(T + 1, k_sq[:], k_ms[:], s_ksq, s_kms)
                merge(Group(T, 2))
                maximum(Group(T, 2))
                mean_square(T + 1, k_ms[:], k_ve[:], s_kms, s_kve)
                low_probs(Group(T, 1))
                if (T + 1).live:
                    dve.wait_ge(s_vh, (T + 2).count())
                    s = (T + 1).slot
                    nc.vector.tensor_tensor(vz_l[:, s, :, HD:2 * HD], ps_b[:, KVDIM:].rearrange("p (g d) -> p g d", g=KV_HEADS),
                                            vz_h[:, s, :, HD:2 * HD].bitcast(F32), ALU.subtract).then_inc(s_vl, 1)
                if (T + 1).live:
                    dve.wait_ge(s_kr, (T + 2).count())
                    wait(dve, s_kt, (T + 1).count())
                    every = [P, KV_HEADS, 2, HD]
                    nc.vector.tensor_tensor(k_nn[:], ps_b[:, 0:KVDIM].rearrange("p (g d) -> p g d", g=KV_HEADS).unsqueeze(2).to_broadcast(every),
                                            k_r[:].unsqueeze(2).unsqueeze(3).to_broadcast(every), ALU.mult).then_inc(s_kn, 1)
                inverse(Group(T, 2))
                low_T(T + 2, s_xth, flat(xT_l), ps_y[:, 2 * P:4 * P], flat(xT_h), s_xtl)
                low_y(Group(T, 0))
                norm_probs(Group(T, 2))
                wait_own(Group(T, 3))
                sum_squares(T + 1, q_sq[1][:], q_ms[:, 8:16], s_qsq[1], s_qms[1])
                merge(Group(T, 3))
                mean_square(T + 1, q_ms[:, 8:16], q_ve[:, 8:16], s_qms[1], s_qve[1])
                maximum(Group(T, 3))
                if (T + 1).live:
                    dve.wait_ge(s_kth, (T + 2).count())
                    c = ((T + 1).slot + 1) * P
                    nc.vector.scalar_tensor_tensor(kT_l[:, :, c:c + P], ps_a[:].rearrange("p (g k) -> p g k", g=KV_HEADS), qk_w[:, 0:1],
                                                   kT_h[:, :, c:c + P].bitcast(F32), op0=ALU.mult, op1=ALU.subtract).then_inc(s_ktl, 1)
                if (T - 1).live:
                    dve.wait_ge(s_o, T.count())
                    nc.vector.tensor_tensor(x1[:], ps_post[:, 0:DIM], xs[:, (T - 1).slot], ALU.add).then_inc(s_x1, 1)
                if (T - 1).live:
                    dve.wait_ge(s_x1, T.count())
                    nc.vector.bn_stats(h_stats[:], x1[:]).then_inc(s_hst, 1)
                low_probs(Group(T, 2))
                if (T - 1).live:
                    dve.wait_ge(s_hst, T.count())
                inverse(Group(T, 3))
                mean_and_var(T - 1, h_stats, h_mv, h_ve, s_hst, s_hmv, s_hve)
                norm_probs(Group(T, 3))
                low_y(Group(T, 1))
                wait_own(Group(T + 1, 0))
                norm_q(T + 1, 1, ps_c)
                if (T - 1).live:
                    dve.wait_ge(s_hrstd, T.count())
                    nc.vector.tensor_scalar(hn[:], x1[:], h_mv[:, 0:1], h_rstd[:, 0:1], ALU.subtract, ALU.mult).then_inc(s_hn, 1)
                merge(Group(T + 1, 0))
                maximum(Group(T + 1, 0))
                if (T + 3).live:
                    dve.wait_ge(s_x[(T + 3).slot], (T + 3).turn(TPS) * 16)
                    nc.vector.bn_stats(x_stats[:], xs[:, (T + 3).slot]).then_inc(s_xst, 1)
                low_T(T - 1, s_hth, flat(hT_l), ps_b, flat(hT_h), s_htl)
                low_probs(Group(T, 3))
                inverse(Group(T + 1, 0))
                low_y(Group(T, 2))
                norm_probs(Group(T + 1, 0))
                if (T + 3).live:
                    dve.wait_ge(s_xst, (T + 4).count())
                wait_own(Group(T + 1, 1))
                if (T - 1).live:
                    dve.wait_ge(s_ffn, T.count())
                    nc.vector.tensor_reduce(g_negmax[:], ps_post[:, DIM + ER:FFN_OUT], AX.X, ALU.max, negate=True).then_inc(s_gmax, 1)
                sum_squares(T + 2, q_sq[0][:], q_ms[:, 0:8], s_qsq[0], s_qms[0])
                merge(Group(T + 1, 1))
                if (T - 1).live:
                    dve.wait_ge(s_gexp, T.count())
                    nc.vector.reciprocal(g_rden[:], g_den[:]).then_inc(s_grd, 1)
                maximum(Group(T + 1, 1))
                if (T - 1).live:
                    dve.wait_ge(s_grd, T.count())
                    nc.vector.tensor_scalar(gate[:], g_exp[:], g_rden[:, 0:1], 1.0 / RANK, ALU.mult, ALU.mult).then_inc(s_gate, 1)
                mean_and_var(T + 3, x_stats, x_mv, x_ve, s_xst, s_xmv, s_xve)
                if (T - 1).live:
                    dve.wait_ge(s_gate, T.count())
                    nc.vector.tensor_tensor(tg[:], ps_post[:, DIM:DIM + ER].rearrange("p (e r) -> p e r", e=EXPERTS),
                                            gate[:].unsqueeze(2).to_broadcast([P, EXPERTS, RANK]), ALU.mult).then_inc(s_tg, 1)
                mean_square(T + 2, q_ms[:, 0:8], q_ve[:, 0:8], s_qms[0], s_qve[0])

            steps(dve, step)

        @block.tensor
        def _(pe):
            def three(ps, stat_h, stat_l, mov_h, mov_l, first, last, onto_ended=False):
                nc.tensor.matmul(ps, stat_h, mov_h, start=first, stop=False, skip_group_check=onto_ended)
                nc.tensor.matmul(ps, stat_l, mov_h, start=False, stop=False, skip_group_check=onto_ended)
                return nc.tensor.matmul(ps, stat_h, mov_l, start=False, stop=last, skip_group_check=onto_ended)

            def transpose_probs(G):
                if G.live:
                    pe.wait_ge(s_pn, G.done())
                    wait(pe, s_pl, G.done(1))
                    for h in range(REP):
                        last = nc.tensor.transpose(ps_pT[:, h], probs[:, G.par, h], ident[:])
                    last.then_inc(s_pt, 1)

            def scores(G):
                if not G.live:
                    return
                T, g = G.tile, G.g
                pe.wait_ge(s_qT, T.count(4, g + 1))
                if g == 0:
                    pe.wait_ge(s_ktl, (T + 1).count())
                wait(pe, s_merged, G.done(1))
                keys = slice(T.slot * P, (T.slot + 2) * P)
                for h in range(REP):
                    q = qT[:, T.par, REP * g + h]
                    nc.tensor.matmul(ps_scores[:, h], q, kT_h[:, g, keys], start=True, stop=False)
                    last = nc.tensor.matmul(ps_scores[:, h], q, kT_l[:, g, keys], start=False, stop=True)
                last.then_inc(s_s, 1)

            def attend(G):
                if not G.live:
                    return
                T, g = G.tile, G.g
                wait(pe, s_yl, G.done(1))
                blocks = [(T.slot, pT_own)] + ([(T.slot - 1, pT_prev)] if T.slot else [])
                pe.wait_ge(s_po, G.done())
                if g == 0:
                    pe.wait_ge(s_vl, (T + 1).count())
                n = 0
                for s, pt in blocks:
                    if n:
                        pe.wait_ge(s_pp, G.prev_done())
                    for half in range(2):
                        cols = slice(HD - HD * half, HD - HD * half + P)
                        vh, vl = vz_h[:, s, g, cols], vz_l[:, s, g, cols]
                        ph, pl = (pt[:, G.par, m, 2 * half:2 * half + 2] for m in range(2))
                        for v, p in ((vh, ph), (vl, ph), (vh, pl)):
                            last = nc.tensor.matmul(ps_y[:, 0:2 * P], v, p, start=n == 0, stop=n == 6 * len(blocks) - 1)
                            n += 1
                last.then_inc(s_pv, 1)

            def project(ps, cols, done):
                for c in range(KC):
                    last = three(ps[:, 0:cols.stop - cols.start], xT_h[:, c], xT_l[:, c], wqkv_h[:, c, cols], wqkv_l[:, c, cols], c == 0, c == KC - 1)
                last.then_inc(done, 1)

            def transpose_q(n, ps):
                for h in range(4):
                    last = nc.tensor.transpose(ps[:, h * P:(h + 1) * P].bitcast(F32R), q_hl[:, 4 * n + h].rearrange("p a d -> p (a d)"), ident_r[:])
                last.then_inc(s_qt, 1)

            pe.wait_ge(s_const, CONSTANTS)
            pe.wait_ge(s_ident_r, 1)

            def project_out(tile, chunks):
                for c in chunks:
                    last = three(ps_post[:, 0:DIM], yT_h[:, tile.par, c], yT_l[:, tile.par, c], wo_h[:, c], wo_l[:, c], c == 0, c == YC - 1)
                if c == YC - 1:
                    last.then_inc(s_o, 1)

            def transpose_block(ps, src, n):
                for c in range(n):
                    last = nc.tensor.transpose(ps[:, c * P:(c + 1) * P], src[:, c * P:(c + 1) * P], ident[:])
                return last

            def step(T):
                if T.k == -2:
                    pe.wait_ge(s_wl, QKV)
                if T.k == 0:
                    pe.wait_ge(s_wl, len(WEIGHTS))
                transpose_probs(Group(T, 0))
                attend(Group(T - 1, 3))
                if T.k == -1:
                    pe.wait_ge(s_zero, 1)
                if (T - 2).live:
                    pe.wait_ge(s_tg, (T - 1).count())
                    wait(pe, s_yl, min_count(T, 4, -1))
                    transpose_block(ps_y[:, 2 * P:], tg[:].rearrange("p e r -> p (e r)"), 1).then_inc(s_tt, 1)
                if (T + 1).live:
                    wait(pe, s_qT, (T + 1).count(4))
                    project(ps_c, slice(BANK, 2 * BANK), s_q[1])
                scores(Group(T, 2))
                if (T - 2).live:
                    pe.wait_ge(s_ttl, (T - 1).count())
                    three(ps_post[:, 0:DIM], tgT_h[:], tgT_l[:], wv_h[:, 0], wv_l[:, 0], False, True, onto_ended=True).then_inc(s_lv, 1)
                if (T + 2).live:
                    pe.wait_ge(s_xn, (T + 3).count())
                    wait(pe, s_yl, T.count(4))
                    transpose_block(ps_y[:, 2 * P:], xn, KC).then_inc(s_xt, 1)
                transpose_probs(Group(T, 1))
                if (T - 1).live:
                    pe.wait_ge(s_yl, T.count(4, -1))
                    wait(pe, s_ob, (T - 1).count())
                    project_out(T - 1, range(0, O_EARLY))
                attend(Group(T, 0))
                scores(Group(T, 3))
                if (T + 1).live:
                    pe.wait_ge(s_kn, (T + 2).count())
                    for g in range(KV_HEADS):
                        last = nc.tensor.transpose(ps_a[:, g * P:(g + 1) * P], k_nn[:, g].rearrange("p a d -> p (a d)"), ident[:])
                    last.then_inc(s_kt, 1)
                if (T - 1).live:
                    pe.wait_ge(s_yl, T.count(4))
                    project_out(T - 1, range(O_EARLY, YC))
                if (T + 1).live:
                    pe.wait_ge(s_vl, (T + 2).count())
                    pe.wait_ge(s_ql[0], (T + 2).count())
                    transpose_q(0, ps_b)
                transpose_probs(Group(T, 2))
                attend(Group(T, 1))
                scores(Group(T + 1, 0))
                if (T + 1).live:
                    transpose_q(1, ps_b)
                if (T + 2).live:
                    wait(pe, s_ktl, (T + 2).count())
                    pe.wait_ge(s_xtl, (T + 3).count())
                    project(ps_a, slice(0, BANK), s_q[0])
                transpose_probs(Group(T, 3))
                if (T - 1).live:
                    pe.wait_ge(s_hn, T.count())
                    wait(pe, s_qT, min_count(T + 1, 4, 2))
                    transpose_block(ps_b, hn, KC).then_inc(s_ht, 1)
                attend(Group(T, 2))
                scores(Group(T + 1, 1))
                if (T + 1).live:
                    pe.wait_ge(s_ql[1], (T + 2).count())
                    pe.wait_ge(s_qT, (T + 1).count(4, 2))
                    wait(pe, s_htl, T.count())
                    transpose_q(2, ps_b)
                if (T - 1).live:
                    pe.wait_ge(s_htl, T.count())
                    for c in range(KC):
                        last = three(ps_post[:, 0:FFN_OUT], hT_h[:, c], hT_l[:, c], wffn_h[:, c], wffn_l[:, c], c == 0, c == KC - 1)
                    last.then_inc(s_ffn, 1)
                if (T + 1).live:
                    transpose_q(3, ps_c)
                if (T + 2).live:
                    wait(pe, s_qT, (T + 1).count(4, 3))
                    project(ps_b, slice(QDIM, QDIM + 2 * KVDIM), s_kv)

            steps(pe, step)

        


def min_count(tile, per=1, more=0):
    n = tile.count(per, more)
    return min(n, TILES * per) if isinstance(n, int) else n


def kernel(L0_attn_x, L0_attn_wq, L0_attn_wk, L0_attn_wv, L0_attn_wo, L0_attn_q_norm_w, L0_attn_k_norm_w,
           L0_ffn_weight, L0_ffn_gate_w, L0_ffn_lora_U, L0_ffn_lora_V):
    import numpy as np
    import concourse.bacc as bacc
    from concourse.bass_utils import run_bass_kernel_spmd

    as_np = np.asarray
    wo = as_np(L0_attn_wo).T.reshape(KV_HEADS, 2, 2, HD, DIM).transpose(0, 2, 1, 3, 4).reshape(QDIM, DIM)
    norm = np.stack([as_np(L0_attn_q_norm_w), as_np(L0_attn_k_norm_w)], axis=1)
    arrays = {
        "x": as_np(L0_attn_x).reshape(SEQS * SEQ_LEN, DIM),
        "w_qkv": np.concatenate([as_np(L0_attn_wq), as_np(L0_attn_wk), as_np(L0_attn_wv)], axis=0).T,
        "w_o": wo,
        "w_ffn": np.concatenate([as_np(L0_ffn_weight), as_np(L0_ffn_lora_U).reshape(ER, DIM), as_np(L0_ffn_gate_w)], axis=0).T,
        "w_v": as_np(L0_ffn_lora_V).transpose(0, 2, 1).reshape(ER, DIM),
        "norm_w": np.concatenate([norm, norm], axis=0),
    }
    arrays = {n: np.ascontiguousarray(a) for n, a in arrays.items()}
    nc = bacc.Bacc("TRN2", target_bir_lowering=False, num_devices=1)
    args = [nc.dram_tensor(n, a.shape, F32, kind="ExternalInput").ap() for n, a in arrays.items()]
    out = nc.dram_tensor("out", [SEQS * SEQ_LEN, DIM], F32, kind="ExternalOutput").ap()
    layer(nc, *args, out)
    r = run_bass_kernel_spmd(nc, [arrays], core_ids=[0])
    return r.results[0]["out"].reshape(SEQS, SEQ_LEN, DIM)
```
